# Optimizing a Trainium2 kernel written in Bass

```python
import numpy as np
import jax
import jax.numpy as jnp

def _softmax(x, axis=-1):
    return jax.nn.softmax(x, axis=axis)

def _gelu(x):
    return jax.nn.gelu(x, approximate=True)

def _silu(x):
    return jax.nn.silu(x)

def _sigmoid(x):
    return jax.nn.sigmoid(x)

def _layernorm(x, axis=-1, eps=1e-05):
    m = jnp.mean(x, axis=axis, keepdims=True)
    v = jnp.var(x, axis=axis, keepdims=True)
    return (x - m) / jnp.sqrt(v + eps)

def _scatter_add(tgt, idx, src, axis=0):
    return tgt.at[idx].add(src)

def _segment_sum(src, seg, n):
    return jax.ops.segment_sum(src, seg, n)
kernel_name = 'mk_adj_resnorm_d2_adj_r2_251bb5'

def setup_inputs(seed: int=0):
    np.random.seed(seed)
    _w = jnp.asarray

    def _rec_inputs():
        import jax
        import jax.numpy as jnp
        _gk = jax.random.key(seed)
        x = -0.0003929 + 0.9999 * jax.random.normal(jax.random.fold_in(_gk, 1), (64, 128, 256), jnp.float32)
        _a = jax.random.bernoulli(jax.random.fold_in(_gk, 2), 0.03125, (64, 128, 128))
        _a = jnp.logical_or(_a, jnp.eye(128, dtype=bool))
        _af = _a.astype(jnp.float32)
        _af = _af * jax.random.uniform(jax.random.fold_in(_gk, 3), (64, 128, 128), jnp.float32, 0.05, 1)
        adj = _af
        return (x, adj)
    x, adj = _rec_inputs()

    def _L0_gnn_setup():
        import jax, jax.numpy as jnp
        import numpy as np
        EPS = 1e-06
        key = jax.random.key(seed)
        k1, k2, k3 = jax.random.split(key, 3)
        B, N, F, O = (8, 2048, 256, 256)
        x = jax.random.normal(k1, (B, N, F), dtype=jnp.float32)
        adj = jax.random.uniform(k2, (B, N, N), dtype=jnp.float32)
        W = jax.random.normal(k3, (O, 2 * F), dtype=jnp.float32) * (1.0 / np.sqrt(2 * F))
        return {'x': x, 'adj': adj, 'W': W}
    _L0_gnn_all = _L0_gnn_setup()
    _L0_gnn_in = {k: v for k, v in _L0_gnn_all.items() if k in ('W',)}
    del _L0_gnn_all

    def _L1_gnn_setup():
        import jax, jax.numpy as jnp
        import numpy as np
        EPS_LN = 1e-05

        def hypergraph_conv(x, adj, W, b):
            N, C, _ = adj.shape
            H = (adj != 0).astype(x.dtype)
            w = adj.reshape(N, -1)[:, :C]
            xw = jnp.einsum('ncd,hd->nch', x, W)
            Dn = jnp.einsum('nce,ne->nc', H, w)
            Dn = jnp.where(Dn > 0, 1.0 / Dn, 0.0)
            Be = H.sum(axis=1)
            Be = jnp.where(Be > 0, 1.0 / Be, 0.0)
            m = Be[:, :, None] * jnp.einsum('nce,nch->neh', H, xw)
            out = Dn[:, :, None] * jnp.einsum('nce,neh->nch', H, m)
            return out + b

        def layer_norm(x, g, b):
            mu = jnp.mean(x, axis=-1, keepdims=True)
            var = jnp.var(x, axis=-1, keepdims=True)
            return (x - mu) * jax.lax.rsqrt(var + EPS_LN) * g + b
        key = jax.random.key(seed)
        ks = jax.random.split(key, 4)
        N, C, Din, Dh, Dout = (16, 512, 256, 512, 256)
        x = jax.random.normal(ks[0], (N, C, Din), dtype=jnp.float32)
        adj = jax.random.uniform(ks[1], (N, C, C), dtype=jnp.float32, minval=0.1, maxval=1.0)
        W1 = jax.random.normal(ks[2], (Dh, Din), dtype=jnp.float32) * (1.0 / np.sqrt(Din))
        b1 = jnp.zeros((Dh,), dtype=jnp.float32)
        gamma = jnp.ones((Dh,), dtype=jnp.float32)
        beta = jnp.zeros((Dh,), dtype=jnp.float32)
        W2 = jax.random.normal(ks[3], (Dout, Dh), dtype=jnp.float32) * (1.0 / np.sqrt(Dh))
        b2 = jnp.zeros((Dout,), dtype=jnp.float32)
        return {'x': x, 'adj': adj, 'W1': W1, 'b1': b1, 'gamma': gamma, 'beta': beta, 'W2': W2, 'b2': b2}
    _L1_gnn_all = _L1_gnn_setup()
    _L1_gnn_in = {k: v for k, v in _L1_gnn_all.items() if k in ('W1', 'b1', 'gamma', 'beta', 'W2', 'b2')}
    del _L1_gnn_all
    return {'x': x, 'adj': adj, 'L0_gnn_W': _L0_gnn_in['W'], 'L1_gnn_W1': _L1_gnn_in['W1'], 'L1_gnn_b1': _L1_gnn_in['b1'], 'L1_gnn_gamma': _L1_gnn_in['gamma'], 'L1_gnn_beta': _L1_gnn_in['beta'], 'L1_gnn_W2': _L1_gnn_in['W2'], 'L1_gnn_b2': _L1_gnn_in['b2']}

def reference(x, adj, L0_gnn_W, L1_gnn_W1, L1_gnn_b1, L1_gnn_gamma, L1_gnn_beta, L1_gnn_W2, L1_gnn_b2):
    import jax
    import jax.numpy as jnp

    def _L0_gnn_ref(x, adj, W):
        import jax, jax.numpy as jnp
        import numpy as np
        EPS = 1e-06
        deg = jnp.sum(adj, axis=-1, keepdims=True)
        agg = jnp.einsum('bij,bjf->bif', adj, x) / jnp.maximum(deg, EPS)
        cat = jnp.concatenate([x, agg], axis=2)
        out = jnp.einsum('bnf,of->bno', cat, W)
        return jax.nn.relu(out)

    def _L1_gnn_ref(x, adj, W1, b1, gamma, beta, W2, b2):
        import jax, jax.numpy as jnp
        import numpy as np
        EPS_LN = 1e-05

        def hypergraph_conv(x, adj, W, b):
            N, C, _ = adj.shape
            H = (adj != 0).astype(x.dtype)
            w = adj.reshape(N, -1)[:, :C]
            xw = jnp.einsum('ncd,hd->nch', x, W)
            Dn = jnp.einsum('nce,ne->nc', H, w)
            Dn = jnp.where(Dn > 0, 1.0 / Dn, 0.0)
            Be = H.sum(axis=1)
            Be = jnp.where(Be > 0, 1.0 / Be, 0.0)
            m = Be[:, :, None] * jnp.einsum('nce,nch->neh', H, xw)
            out = Dn[:, :, None] * jnp.einsum('nce,neh->nch', H, m)
            return out + b

        def layer_norm(x, g, b):
            mu = jnp.mean(x, axis=-1, keepdims=True)
            var = jnp.var(x, axis=-1, keepdims=True)
            return (x - mu) * jax.lax.rsqrt(var + EPS_LN) * g + b
        h = jax.nn.relu(hypergraph_conv(x, adj, W1, b1))
        h = layer_norm(h, gamma, beta)
        y = hypergraph_conv(h, adj, W2, b2)
        return y + x
    x = _layernorm(x + _L0_gnn_ref(x, adj, L0_gnn_W), axis=-1)
    x = _layernorm(x + _L1_gnn_ref(x, adj, L1_gnn_W1, L1_gnn_b1, L1_gnn_gamma, L1_gnn_beta, L1_gnn_W2, L1_gnn_b2), axis=-1)
    return x

_drawn_inputs = setup_inputs


def setup_inputs(seed=0):
    import zlib

    import numpy as np

    out = dict(_drawn_inputs(seed))
    spreads = {'L1_gnn_b1': (0.0, 0.1),
     'L1_gnn_gamma': (1.0, 0.2),
     'L1_gnn_beta': (0.0, 0.1),
     'L1_gnn_b2': (0.0, 0.1)}
    factors = {}
    for name, (base, spread) in spreads.items():
        noise = np.random.default_rng([zlib.crc32(name.encode()), seed]).standard_normal(out[name].shape)
        drawn = base * np.exp(spread * noise) if base else spread * noise
        out[name] = jnp.asarray(drawn.astype(out[name].dtype))
    for name, factor in factors.items():
        out[name] = (out[name] * factor).astype(out[name].dtype)
    return out
```

```python
import concourse.bass as bass
from concourse import mybir
from contextlib import ExitStack


def gnn_hypergraph_kernel(nc: bass.Bass, x: bass.AP, adj: bass.AP, gnn_w: bass.AP, w1: bass.AP,
                          b1: bass.AP, gamma: bass.AP, beta: bass.AP, w2: bass.AP, b2: bass.AP,
                          out: bass.AP):
    fp32 = mybir.dt.float32
    bf16 = mybir.dt.bfloat16
    ALU = mybir.AluOpType
    ACT = mybir.ActivationFunctionType
    AX = mybir.AxisListType

    GRAPHS, P, D = x.shape
    HID = w1.shape[0]
    KD = D // P
    KH = HID // P
    PAIRS = GRAPHS // 2
    EPS_DEG = 1e-6
    EPS_LN = 1e-5
    TINY = 1.17549435e-38
    STAT = D + 2

    x_d = x.rearrange("(n g) p d -> n p g d", g=2)
    adj_d = adj.rearrange("(n g) p e -> n p g e", g=2)
    out_d = out.rearrange("(n g) p d -> n p g d", g=2)

    ctx = ExitStack()
    with ctx:
        def sb(name, shape, dt=fp32):
            return ctx.enter_context(nc.sbuf_tensor(name, shape, dt))

        def sem(name):
            return ctx.enter_context(nc.semaphore(name))

        ident = sb("ident", [P, P])
        ident_bf = sb("ident_bf", [P, P], bf16)
        ones_col = sb("ones_col", [P, 2])
        ones_bf = sb("ones_bf", [P, 2], bf16)
        hid_mean = sb("hid_mean", [P, P])
        minus_half = sb("minus_half", [P, 2])
        floors = sb("floors", [P, 4])
        w0_raw = sb("w0_raw", [P, D // P, 2 * D])
        w1_raw = sb("w1_raw", [P, KH, D])
        w2_raw = sb("w2_raw", [P, D // P, HID])
        wab = sb("wab", [P, KD, 2 * D])
        w1t = sb("w1t", [P, KD, HID])
        w2t = sb("w2t", [P, KH, D])
        w2c = sb("w2c", [P, KH, D + 2])
        b1_col = sb("b1_col", [P, KH])
        gamma_col = sb("gamma_col", [P, KH])
        beta_col = sb("beta_col", [P, KH])
        beta_wide = sb("beta_wide", [P, KH, P])
        b2_rows = sb("b2_rows", [P, D])
        b2_half = sb("b2_half", [P, D])
        beta_w2 = sb("beta_w2", [P, D])
        x_sb = sb("x_sb", [P, 2, 2, D])
        adj_sb = sb("adj_sb", [P, 2, 2, P])
        hub_sb = sb("hub_sb", [P, 2, 2, P])
        sums = sb("sums", [P, 4])
        safe = sb("safe", [P, 4])
        recips = sb("recips", [P, 4])
        dn = sb("dn", [P, 2])
        picked = sb("picked", [P, 2, P])
        edges = sb("edges", [P, 2, P], bf16)
        adj_n = sb("adj_n", [P, 2, P])
        edges_dn = sb("edges_dn", [P, 2, P])
        adj_t = sb("adj_t", [P, 2, 2, P])
        edges_dn_t = sb("edges_dn_t", [P, 2, P])
        counts = sb("counts", [P, 2])
        be = sb("be", [P, 2])
        edges_be_t = sb("edges_be_t", [P, 2, P])
        g_sb = sb("g_sb", [P, 2, 2, P])
        x_t = sb("x_t", [P, 2, KD, P])
        yb_sb = sb("yb_sb", [P, 2, D])
        pre1 = sb("pre1", [P, 2, D])
        stats1 = sb("stats1", [P, 2, 6])
        mv1 = sb("mv1", [P, 2, 2])
        veps1 = sb("veps1", [P, 2])
        rstd1 = sb("rstd1", [P, 2])
        x1 = sb("x1", [P, 2, D])
        x1_b2 = sb("x1_b2", [P, 2, 2, D])
        u_t = sb("u_t", [P, KD, 2, P])
        h = sb("h", [P, KH, 2, P])
        h_sq = sb("h_sq", [P, KH, 2, P])
        h_sq2 = sb("h_sq2", [P, KH // 2, 2, P])
        h_sq1 = sb("h_sq1", [P, 2, P])
        hsum = sb("hsum", [P, 2, 2])
        mean_sq = sb("mean_sq", [P, 2])
        var_h = sb("var_h", [P, 2])
        veps_h = sb("veps_h", [P, 2])
        rstd_h = sb("rstd_h", [P, 2])
        q_sb = sb("q_sb", [P, 2, D])
        pre2 = sb("pre2", [P, 2, D])
        stats2 = sb("stats2", [P, 2, 6])
        mv2 = sb("mv2", [P, 2, 2])
        veps2 = sb("veps2", [P, 2])
        rstd2 = sb("rstd2", [P, 2])
        out_sb = sb("out_sb", [P, 2, 2, D])

        bank = [ctx.enter_context(nc.psum_tensor(f"bank{i}", [P, 512], fp32)) for i in range(8)]
        ps_adj_t = bank[0][:, 0:2 * P]
        ps_edn_t = bank[0][:, 2 * P:4 * P]
        ps_edges_t = bank[1][:, 0:P].bitcast(bf16)
        ps_counts = bank[1][:, P:P + 2]
        ps_g = bank[1][:, 2 * P:4 * P]
        ps_x_t = bank[2]
        ps_y = [bank[3], bank[4]]
        ps_u_t = bank[5]
        ps_f = bank[5]
        ps_z = [bank[6], bank[7]]
        ps_q = [bank[6], bank[7]]

        s_weights_in = sem("weights_in")
        s_consts = sem("consts")
        s_setup_pe = sem("setup_pe")
        s_setup_dve = sem("setup_dve")
        s_x_in = [sem(f"x_in{i}") for i in range(2)]
        s_adj_in = [sem(f"adj_in{i}") for i in range(2)]
        s_stored = [sem(f"stored{i}") for i in range(2)]
        s_sums = sem("sums_ready")
        s_safe = sem("safe_ready")
        s_recips = sem("recips_ready")
        s_dn = sem("dn_ready")
        s_prep = sem("prep_ready")
        s_adj_ps = sem("adj_transposed")
        s_adj_t = sem("adj_t_ready")
        s_edn_t = sem("edges_dn_t_ready")
        s_counts = sem("counts_ready")
        s_be = sem("be_ready")
        s_ebe_t = sem("edges_be_t_ready")
        s_g_ps = sem("g_in_psum")
        s_g = sem("g_ready")
        s_x_ps = sem("x_transposed")
        s_x_t = sem("x_t_ready")
        s_y_ps = sem("y_in_psum")
        s_yb = sem("yb_ready")
        s_p_ps = sem("p_in_psum")
        s_pre1 = sem("pre1_ready")
        s_stats1 = sem("stats1_ready")
        s_mv1 = sem("mv1_ready")
        s_veps1 = sem("veps1_ready")
        s_rstd1 = sem("rstd1_ready")
        s_x1 = sem("x1_ready")
        s_x1_b2 = sem("x1_b2_ready")
        s_u_ps = sem("u_in_psum")
        s_u_t = sem("u_t_ready")
        s_z_ps = sem("z_in_psum")
        s_h = sem("h_ready")
        s_h_sq = sem("h_sq_ready")
        s_h_sq2 = sem("h_sq2_ready")
        s_h_sq1 = sem("h_sq1_ready")
        s_q_ps = sem("q_in_psum")
        s_hsum = sem("hsum_ready")
        s_mean_sq = sem("mean_sq_ready")
        s_var_h = sem("var_h_ready")
        s_veps_h = sem("veps_h_ready")
        s_rstd_h = sem("rstd_h_ready")
        s_q = sem("q_ready")
        s_f_ps = sem("f_in_psum")
        s_pre2 = sem("pre2_ready")
        s_stats2 = sem("stats2_ready")
        s_mv2 = sem("mv2_ready")
        s_veps2 = sem("veps2_ready")
        s_rstd2 = sem("rstd2_ready")
        s_out = sem("out_ready")

        def nth(i, c, per=1, k=0):
            return 2 * per * i + (per * c + k + 1)

        def loads(i, c):
            return 16 * i + 16 * (c // 2 + 1)

        def run(eng, step):
            step(0, 0)
            step(0, 1)
            with eng.Fori(1, PAIRS // 2 - 2) as i:
                step(i, 0)
                step(i, 1)
            for t in range(PAIRS - 4, PAIRS + 2):
                step(0, t)

        def live(i, c):
            return not isinstance(i, int) or 0 <= c < PAIRS

        def later(i, c, least):
            return not isinstance(i, int) or c >= least

        block = ctx.enter_context(nc.Block())

        @block.sync
        def _(sp):
            def load_adj(i, c):
                slot = c % 2
                if later(i, c, 2):
                    sp.wait_ge(s_prep, nth(i, c - 2, 3, 2))
                sp.dma_start(adj_sb[:, slot], adj_d[2 * i + c]).then_inc(s_adj_in[slot], 16)
                for g in range(2):
                    row = adj_d[2 * i + c, 0:1, g, :].to_broadcast([P, P])
                    sp.dma_start(hub_sb[:, slot, g], row).then_inc(s_adj_in[slot], 16)

            def load_x(i, c):
                slot = c % 2
                if later(i, c, 2):
                    sp.wait_ge(s_pre1, nth(i, c - 2, 2, 1))
                sp.dma_start(x_sb[:, slot], x_d[2 * i + c]).then_inc(s_x_in[slot], 16)

            load_x(0, 0)
            load_adj(0, 0)
            sp.dma_start(w0_raw[:, :, :], gnn_w.rearrange("(b p) f -> p b f", p=P)).then_inc(s_weights_in, 16)
            sp.dma_start(w1_raw[:, :, :], w1.rearrange("(b p) f -> p b f", p=P)).then_inc(s_weights_in, 16)
            sp.dma_start(w2_raw[:, :, :], w2.rearrange("(b p) f -> p b f", p=P)).then_inc(s_weights_in, 16)
            with nc.allow_non_contiguous_dma(reason="three vectors of 512, once"):
                for col, vec in ((b1_col, b1), (gamma_col, gamma), (beta_col, beta)):
                    sp.dma_start(col[:, :], vec.rearrange("(k p) -> p k", p=P)).then_inc(s_weights_in, 16)
            sp.dma_start(b2_rows[:, :], b2.rearrange("(a d) -> a d", a=1).to_broadcast([P, D])).then_inc(s_weights_in, 16)
            load_x(0, 1)
            load_adj(0, 1)
            load_adj(0, 2)

            def step(i, c):
                if live(i, c + 3):
                    load_adj(i, c + 3)
                if live(i, c - 2):
                    sp.wait_ge(s_out, nth(i, c - 2, 2, 1))
                    sp.dma_start(out_d[2 * i + (c - 2)], out_sb[:, c % 2]).then_inc(s_stored[c % 2], 16)
                if live(i, c + 2):
                    load_x(i, c + 2)
            run(sp, step)
            for slot in range(2):
                sp.wait_ge(s_stored[slot], 16 * (PAIRS // 2))

        @block.gpsimd
        def _(pool):
            nc.gpsimd.memset(ident[:, :], 0.0).then_inc(s_consts, 1)
            nc.gpsimd.memset(ident_bf[:, :], 0.0).then_inc(s_consts, 1)
            nc.gpsimd.memset(ones_col[:, :], 1.0).then_inc(s_consts, 1)
            nc.gpsimd.memset(ones_bf[:, :], 1.0).then_inc(s_consts, 1)
            nc.gpsimd.memset(hid_mean[:, :], 1.0 / HID).then_inc(s_consts, 1)
            nc.gpsimd.memset(minus_half[:, :], -0.5).then_inc(s_consts, 1)
            nc.gpsimd.memset(floors[:, 0:2], EPS_DEG).then_inc(s_consts, 1)
            nc.gpsimd.memset(floors[:, 2:4], TINY).then_inc(s_consts, 1)
            nc.gpsimd.memset(w2c[:, :, D:D + 2], 1.0).then_inc(s_consts, 1)
            pool.wait_ge(s_consts, 9)
            for m in (ident, ident_bf):
                nc.gpsimd.affine_select(out=m[:, :], in_=m[:, :], compare_op=ALU.not_equal, fill=1.0,
                                        base=0, pattern=[[-1, P]], channel_multiplier=1).then_inc(s_consts, 1)
            pool.wait_ge(s_consts, 11)
            pool.wait_ge(s_setup_dve, 1)

            def inverse_root(i, c, rstd, veps, s_veps, s_rstd):
                pool.wait_ge(s_veps, nth(i, c))
                nc.gpsimd.tensor_tensor(rstd[:, :], veps[:, :], minus_half[:, :], ALU.pow).then_inc(s_rstd, 1)

            def step(i, c):
                if live(i, c - 2):
                    inverse_root(i, c - 2, rstd2, veps2, s_veps2, s_rstd2)
                if live(i, c - 1):
                    pool.wait_ge(s_h_sq, nth(i, c - 1, 2, 1))
                    nc.gpsimd.tensor_tensor(h_sq2[:, :], h_sq[:, 0:2], h_sq[:, 2:4], ALU.add).then_inc(s_h_sq2, 1)
                    pool.wait_ge(s_h_sq2, nth(i, c - 1))
                    nc.gpsimd.tensor_tensor(h_sq1[:, :], h_sq2[:, 0], h_sq2[:, 1], ALU.add).then_inc(s_h_sq1, 1)
                if live(i, c):
                    inverse_root(i, c, rstd1, veps1, s_veps1, s_rstd1)
                    pool.wait_ge(s_x1, nth(i, c, 2, 1))
                    if later(i, c, 2):
                        pool.wait_ge(s_pre2, nth(i, c - 2, 2, 1))
                    for g in range(2):
                        nc.gpsimd.tensor_tensor(x1_b2[:, c % 2, g], x1[:, g], b2_half[:, :], ALU.add)\
                            .then_inc(s_x1_b2, 1)
                if live(i, c - 1):
                    inverse_root(i, c - 1, rstd_h, veps_h, s_veps_h, s_rstd_h)
            run(pool, step)

        @block.scalar
        def _(act):
            def copy_adj_t(i, c):
                act.wait_ge(s_adj_ps, nth(i, c))
                nc.scalar.activation(adj_t[:, c % 2], ps_adj_t, ACT.Copy).then_inc(s_adj_t, 1)
                nc.scalar.activation(edges_dn_t[:, :], ps_edn_t, ACT.Copy).then_inc(s_edn_t, 1)

            def copy_x_t(i, c):
                act.wait_ge(s_x_ps, nth(i, c))
                nc.scalar.activation(x_t[:, :], ps_x_t[:, :], ACT.Copy).then_inc(s_x_t, 1)

            def step(i, c):
                if live(i, c - 1):
                    act.wait_ge(s_u_ps, nth(i, c - 1))
                    nc.scalar.activation(u_t[:, :], ps_u_t[:, :], ACT.Copy).then_inc(s_u_t, 1)
                if live(i, c):
                    for g in range(2):
                        act.wait_ge(s_y_ps, nth(i, c, 2, g))
                        nc.scalar.activation(yb_sb[:, g], ps_y[g][:, D:2 * D], ACT.Copy).then_inc(s_yb, 1)
                    act.wait_ge(s_g_ps, nth(i, c))
                    nc.scalar.activation(g_sb[:, c % 2], ps_g, ACT.Copy).then_inc(s_g, 1)
                if live(i, c - 1):
                    for m in range(KH):
                        act.wait_ge(s_z_ps, nth(i, c - 1, KH, m | 1))
                        nc.scalar.activation(h[:, m], ps_z[m // 2][:, (m % 2) * 2 * P:(m % 2 + 1) * 2 * P],
                                             ACT.Relu, bias=b1_col[:, m:m + 1]).then_inc(s_h, 1)
                        if m % 2:
                            act.wait_ge(s_h, nth(i, c - 1, KH, m))
                            nc.scalar.activation(h_sq[:, m - 1:m + 1], h[:, m - 1:m + 1], ACT.Square)\
                                .then_inc(s_h_sq, 1)
                if live(i, c + 1):
                    copy_x_t(i, c + 1)
                    copy_adj_t(i, c + 1)

            act.wait_ge(s_setup_dve, 2)
            copy_x_t(0, 0)
            copy_adj_t(0, 0)
            run(act, step)

        @block.vector
        def _(dve):
            dve.wait_ge(s_weights_in, 16 * 7)
            nc.vector.tensor_scalar(b2_half[:, :], b2_rows[:, :], 0.5, None, ALU.mult).then_inc(s_setup_dve, 1)
            nc.vector.tensor_copy(beta_wide[:, :, :], beta_col[:, :].unsqueeze(2).to_broadcast([P, KH, P]))\
                .then_inc(s_setup_dve, 1)
            outs = [wab[:, k, f * D:(f + 1) * D] for f in range(2) for k in range(KD)]
            outs += [w1t[:, k, :] for k in range(KD)]
            outs += [w2t[:, k, :] for k in range(KH)]
            for n, o in enumerate(outs):
                dve.wait_ge(s_setup_pe, n + 1)
                nc.vector.tensor_copy(o, bank[n % 8][:, 0:o.free_size()]).then_inc(s_setup_dve, 1)
            done = 2 + len(outs)
            dve.wait_ge(s_setup_dve, done)
            for k in range(KH):
                nc.vector.tensor_scalar(w2c[:, k, 0:D], w2t[:, k, :], gamma_col[:, k:k + 1], None, ALU.mult)\
                    .then_inc(s_setup_dve, 1)
            done += KH
            dve.wait_ge(s_setup_pe, len(outs) + 1)
            nc.vector.tensor_copy(beta_w2[:, :], bank[6][:, 0:D]).then_inc(s_setup_dve, 1)
            dve.wait_ge(s_setup_pe, len(outs) + 2)
            dve.wait_ge(s_setup_dve, done + 1)
            for k in range(KH):
                nc.vector.tensor_tensor(w2c[:, k, 0:D], w2c[:, k, 0:D], bank[7][:, 0:D], ALU.subtract)\
                    .then_inc(s_setup_dve, 1)
            dve.wait_ge(s_consts, 11)

            def prepare(i, c):
                slot = c % 2
                a = adj_sb[:, slot]
                dve.wait_ge(s_adj_in[slot], 3 * loads(i, c))
                nc.vector.tensor_reduce(sums[:, 0:2], a, AX.X, ALU.add).then_inc(s_sums, 1)
                for g in range(2):
                    nc.vector.scalar_tensor_tensor(
                        out=picked[:, g], in0=adj_sb[:, slot, g], scalar=0.0, in1=hub_sb[:, slot, g],
                        op0=ALU.not_equal, op1=ALU.mult, accum_out=sums[:, 2 + g:3 + g]).then_inc(s_sums, 1)
                if later(i, c, 1):
                    dve.wait_ge(s_adj_ps, nth(i, c - 1))
                nc.vector.tensor_scalar(edges[:, :], a, 0.0, None, ALU.not_equal).then_inc(s_prep, 1)
                dve.wait_ge(s_sums, nth(i, c, 3, 2))
                nc.vector.tensor_tensor(safe[:, :], sums[:, :], floors[:, :], ALU.max).then_inc(s_safe, 1)
                dve.wait_ge(s_safe, nth(i, c))
                nc.vector.reciprocal(recips[:, :], safe[:, :]).then_inc(s_recips, 1)
                dve.wait_ge(s_recips, nth(i, c))
                nc.vector.scalar_tensor_tensor(out=dn[:, :], in0=sums[:, 2:4], scalar=0.0, in1=recips[:, 2:4],
                                               op0=ALU.is_gt, op1=ALU.mult).then_inc(s_dn, 1)
                nc.vector.tensor_tensor(adj_n[:, :], a, recips[:, 0:2].unsqueeze(2).to_broadcast([P, 2, P]),
                                        ALU.mult).then_inc(s_prep, 1)
                dve.wait_ge(s_dn, nth(i, c))
                nc.vector.tensor_tensor(edges_dn[:, :], edges[:, :], dn[:, :].unsqueeze(2).to_broadcast([P, 2, P]),
                                        ALU.mult).then_inc(s_prep, 1)

            def scale_edges(i, c):
                dve.wait_ge(s_adj_ps, nth(i, c))
                nc.vector.tensor_scalar(counts[:, :], ps_counts, 1.0, None, ALU.max).then_inc(s_counts, 1)
                dve.wait_ge(s_counts, nth(i, c))
                nc.vector.reciprocal(be[:, :], counts[:, :]).then_inc(s_be, 1)
                dve.wait_ge(s_be, nth(i, c))
                nc.vector.tensor_tensor(edges_be_t[:, :], ps_edges_t.rearrange("p (g e) -> p g e", g=2),
                                        be[:, :].unsqueeze(2).to_broadcast([P, 2, P]), ALU.mult)\
                    .then_inc(s_ebe_t, 1)

            def gather(i, c, pre, stats, s_pre, s_stats):
                for g in range(2):
                    dve.wait_ge(s_pre, nth(i, c, 2, g))
                    nc.vector.bn_stats(stats[:, g], pre[:, g]).then_inc(s_stats, 1)
                dve.wait_ge(s_stats, nth(i, c, 2, 1))

            def merge(i, c, stats, mv, veps, s_mv, s_veps):
                for g in range(2):
                    nc.vector.bn_aggr(mv[:, g], stats[:, g]).then_inc(s_mv, 1)
                dve.wait_ge(s_mv, nth(i, c, 2, 1))
                nc.vector.tensor_scalar(veps[:, :], mv[:, :, 1], EPS_LN, None, ALU.add).then_inc(s_veps, 1)

            def step(i, c):
                if live(i, c - 2):
                    dve.wait_ge(s_rstd_h, nth(i, c - 2))
                    for g in range(2):
                        nc.vector.scalar_tensor_tensor(
                            out=q_sb[:, g], in0=ps_q[g][:, 0:D], scalar=rstd_h[:, g:g + 1], in1=beta_w2[:, :],
                            op0=ALU.mult, op1=ALU.add).then_inc(s_q, 1)
                if live(i, c - 2):
                    dve.wait_ge(s_x1_b2, nth(i, c - 2, 2, 1))
                    dve.wait_ge(s_f_ps, nth(i, c - 2))
                    for g in range(2):
                        nc.vector.scalar_tensor_tensor(
                            out=pre2[:, g], in0=x1_b2[:, c % 2, g], scalar=2.0, in1=ps_f[:, g * D:(g + 1) * D],
                            op0=ALU.mult, op1=ALU.add).then_inc(s_pre2, 1)
                    gather(i, c - 2, pre2, stats2, s_pre2, s_stats2)
                if live(i, c + 1):
                    prepare(i, c + 1)
                if live(i, c - 2):
                    merge(i, c - 2, stats2, mv2, veps2, s_mv2, s_veps2)
                if live(i, c):
                    dve.wait_ge(s_x_in[c % 2], loads(i, c))
                    for g in range(2):
                        dve.wait_ge(s_p_ps, nth(i, c, 2, g))
                        nc.vector.scalar_tensor_tensor(
                            out=pre1[:, g], in0=ps_y[g][:, 0:D], scalar=0.0, in1=x_sb[:, c % 2, g],
                            op0=ALU.max, op1=ALU.add).then_inc(s_pre1, 1)
                    gather(i, c, pre1, stats1, s_pre1, s_stats1)
                if live(i, c + 1):
                    scale_edges(i, c + 1)
                if live(i, c):
                    merge(i, c, stats1, mv1, veps1, s_mv1, s_veps1)
                if live(i, c - 2):
                    dve.wait_ge(s_rstd2, nth(i, c - 2))
                    if later(i, c - 2, 2):
                        dve.wait_ge(s_stored[c % 2], loads(i, c - 4))
                    for g in range(2):
                        nc.vector.tensor_scalar(out_sb[:, c % 2, g], pre2[:, g], mv2[:, g, 0:1], rstd2[:, g:g + 1],
                                                ALU.subtract, ALU.mult).then_inc(s_out, 1)
                if live(i, c):
                    dve.wait_ge(s_rstd1, nth(i, c))
                    if later(i, c, 1):
                        dve.wait_ge(s_x1_b2, nth(i, c - 1, 2, 1))
                    for g in range(2):
                        nc.vector.tensor_scalar(x1[:, g], pre1[:, g], mv1[:, g, 0:1], rstd1[:, g:g + 1],
                                                ALU.subtract, ALU.mult).then_inc(s_x1, 1)
                if live(i, c - 1):
                    dve.wait_ge(s_q_ps, nth(i, c - 1))
                    for g in range(2):
                        nc.vector.tensor_copy(hsum[:, g], ps_q[g][:, D:D + 3:2]).then_inc(s_hsum, 1)
                    dve.wait_ge(s_hsum, nth(i, c - 1, 2, 1))
                    nc.vector.scalar_tensor_tensor(out=mean_sq[:, :], in0=hsum[:, :, 0], scalar=1.0 / HID ** 2,
                                                   in1=hsum[:, :, 0], op0=ALU.mult, op1=ALU.mult).then_inc(s_mean_sq, 1)
                    dve.wait_ge(s_mean_sq, nth(i, c - 1))
                    nc.vector.scalar_tensor_tensor(out=var_h[:, :], in0=hsum[:, :, 1], scalar=1.0 / HID,
                                                   in1=mean_sq[:, :], op0=ALU.mult, op1=ALU.subtract).then_inc(s_var_h, 1)
                    dve.wait_ge(s_var_h, nth(i, c - 1))
                    nc.vector.tensor_scalar(veps_h[:, :], var_h[:, :], 0.0, EPS_LN, ALU.max, ALU.add).then_inc(s_veps_h, 1)

            prepare(0, 0)
            scale_edges(0, 0)
            run(dve, step)

        @block.tensor
        def _(pe):
            mm = nc.tensor.matmul
            pe.wait_ge(s_consts, 11)
            pe.wait_ge(s_weights_in, 16 * 7)
            jobs = [[w0_raw[:, b, f * D + k * P:f * D + (k + 1) * P] for b in range(D // P)]
                    for f in range(2) for k in range(KD)]
            jobs += [[w1_raw[:, b, k * P:(k + 1) * P] for b in range(KH)] for k in range(KD)]
            jobs += [[w2_raw[:, b, k * P:(k + 1) * P] for b in range(D // P)] for k in range(KH)]
            for n, job in enumerate(jobs):
                if n >= 8:
                    pe.wait_ge(s_setup_dve, 2 + n - 7)
                for b, src in enumerate(job):
                    last = nc.tensor.transpose(bank[n % 8][:, b * P:(b + 1) * P], src, ident[:, :])
                last.then_inc(s_setup_pe, 1)
            pe.wait_ge(s_setup_dve, 2 + len(jobs))
            for k in range(KH):
                last = mm(bank[6][:, 0:D], beta_wide[:, k, :], w2t[:, k, :], start=(k == 0), stop=(k == KH - 1))
            last.then_inc(s_setup_pe, 1)
            pe.wait_ge(s_setup_dve, 2 + len(jobs) + KH)
            for k in range(KH):
                last = mm(bank[7][:, 0:D], hid_mean[:, :], w2c[:, k, 0:D], start=(k == 0), stop=(k == KH - 1))
            last.then_inc(s_setup_pe, 1)

            def turn_x(i, c):
                slot = c % 2
                pe.wait_ge(s_x_in[slot], loads(i, c))
                if later(i, c, 1):
                    pe.wait_ge(s_x_t, nth(i, c - 1))
                for g in range(2):
                    for k in range(KD):
                        last = nc.tensor.transpose(ps_x_t[:, (g * KD + k) * P:(g * KD + k + 1) * P],
                                                   x_sb[:, slot, g, k * P:(k + 1) * P], ident[:, :])
                last.then_inc(s_x_ps, 1)

            def turn_adj(i, c):
                pe.wait_ge(s_prep, nth(i, c, 3, 2))
                if later(i, c, 1):
                    pe.wait_ge(s_adj_t, nth(i, c - 1))
                    pe.wait_ge(s_edn_t, nth(i, c - 1))
                    pe.wait_ge(s_g, nth(i, c - 1))
                for g in range(2):
                    nc.tensor.transpose(ps_adj_t[:, g * P:(g + 1) * P], adj_n[:, g], ident[:, :])
                    nc.tensor.transpose(ps_edn_t[:, g * P:(g + 1) * P], edges_dn[:, g], ident[:, :])
                    nc.tensor.transpose(ps_edges_t[:, g * P:(g + 1) * P], edges[:, g], ident_bf[:, :])
                    last = mm(ps_counts[:, g:g + 1], edges[:, g], ones_bf[:, 0:1], start=True, stop=True)
                last.then_inc(s_adj_ps, 1)

            def step(i, c):
                if live(i, c):
                    pe.wait_ge(s_x_t, nth(i, c))
                    for g in range(2):
                        if later(i, c, 1):
                            pe.wait_ge(s_pre1, nth(i, c - 1, 2, g))
                        for k in range(KD):
                            last = mm(ps_y[g][:, :], x_t[:, g, k, :], wab[:, k, :], start=(k == 0), stop=(k == KD - 1))
                        last.then_inc(s_y_ps, 1)
                if live(i, c - 2):
                    pe.wait_ge(s_u_t, nth(i, c - 1) if live(i, c - 1) else nth(i, c - 2))
                    for g in range(2):
                        pe.wait_ge(s_q, nth(i, c - 2, 2, g))
                        last = mm(ps_f[:, g * D:(g + 1) * D], g_sb[:, c % 2, g, :], q_sb[:, g, :],
                                  start=True, stop=True)
                    last.then_inc(s_f_ps, 1)
                if live(i, c):
                    pe.wait_ge(s_ebe_t, nth(i, c))
                    pe.wait_ge(s_edn_t, nth(i, c))
                    for g in range(2):
                        last = mm(ps_g[:, g * P:(g + 1) * P], edges_be_t[:, g, :], edges_dn_t[:, g, :],
                                  start=True, stop=True)
                    last.then_inc(s_g_ps, 1)
                if live(i, c - 1):
                    pe.wait_ge(s_u_t, nth(i, c - 1))
                    if later(i, c - 1, 1):
                        pe.wait_ge(s_q, nth(i, c - 2, 2, 1))
                    for m in range(KH):
                        for k in range(KD):
                            last = mm(ps_z[m // 2][:, (m % 2) * 2 * P:(m % 2 + 1) * 2 * P],
                                      w1t[:, k, m * P:(m + 1) * P], u_t[:, k], start=(k == 0), stop=(k == KD - 1))
                        last.then_inc(s_z_ps, 1)
                if live(i, c):
                    pe.wait_ge(s_adj_t, nth(i, c))
                    for g in range(2):
                        pe.wait_ge(s_yb, nth(i, c, 2, g))
                        mm(ps_y[g][:, 0:D], adj_t[:, c % 2, g, :], yb_sb[:, g, :], start=False, stop=True,
                           skip_group_check=True)\
                            .then_inc(s_p_ps, 1)
                if live(i, c + 1):
                    turn_x(i, c + 1)
                    turn_adj(i, c + 1)
                if live(i, c - 1):
                    pe.wait_ge(s_h, nth(i, c - 1, KH, KH - 1))
                    for g in range(2):
                        for m in range(KH):
                            mm(ps_q[g][:, 0:D + 2], h[:, m, g, :], w2c[:, m, :], start=(m == 0), stop=(m == KH - 1))
                    pe.wait_ge(s_h_sq1, nth(i, c - 1))
                    for g in range(2):
                        last = mm(ps_q[g][:, STAT:STAT + 1], h_sq1[:, g, :], ones_col[:, 0:1], start=True, stop=True)
                    last.then_inc(s_q_ps, 1)
                if live(i, c):
                    pe.wait_ge(s_g, nth(i, c))
                    if later(i, c, 2):
                        pe.wait_ge(s_pre2, nth(i, c - 2, 2, 1))
                    for g in range(2):
                        pe.wait_ge(s_x1, nth(i, c, 2, g))
                        for k in range(KD):
                            last = mm(ps_u_t[:, (k * 2 + g) * P:(k * 2 + g + 1) * P], x1[:, g, k * P:(k + 1) * P],
                                      g_sb[:, c % 2, g, :], start=True, stop=True)
                    last.then_inc(s_u_ps, 1)

            pe.wait_ge(s_setup_dve, 2 + len(jobs) + 2 * KH + 1)
            turn_x(0, 0)
            turn_adj(0, 0)
            run(pe, step)


_INS = ['x', 'adj', 'L0_gnn_W', 'L1_gnn_W1', 'L1_gnn_b1', 'L1_gnn_gamma', 'L1_gnn_beta', 'L1_gnn_W2', 'L1_gnn_b2']
_OUTS = [((64, 128, 256), 'float32')]


def kernel(**inputs):
    import numpy as _np
    import concourse.bacc as _bacc
    from concourse import mybir as _mybir
    from concourse.bass_utils import run_bass_kernel_spmd as _run

    nc = _bacc.Bacc("TRN2", target_bir_lowering=False, num_devices=1)
    arrays, args = {}, []
    for name in _INS:
        a = _np.ascontiguousarray(inputs[name])
        arrays[f"in_{name}_dram"] = a
        args.append(nc.dram_tensor(f"in_{name}_dram", a.shape, _mybir.dt.from_np(a.dtype), kind="ExternalInput").ap())
    for i, (shape, dtype) in enumerate(_OUTS):
        dt = _mybir.dt.from_np(_np.dtype(dtype))
        args.append(nc.dram_tensor(f"out_{i}_dram", shape, dt, kind="ExternalOutput").ap())
    gnn_hypergraph_kernel(nc, *args)
    r = _run(nc, [arrays], core_ids=[0])
    got = tuple(r.results[0][f"out_{i}_dram"] for i in range(len(_OUTS)))
    return got[0]
```

```python
import concourse.bass as bass
from concourse import mybir
from contextlib import ExitStack


def gnn_hypergraph_kernel(nc: bass.Bass, x: bass.AP, adj: bass.AP, gnn_w: bass.AP, w1: bass.AP,
                          b1: bass.AP, gamma: bass.AP, beta: bass.AP, w2: bass.AP, b2: bass.AP,
                          out: bass.AP):
    fp32 = mybir.dt.float32
    fp32r = mybir.dt.float32r
    bf16 = mybir.dt.bfloat16
    ALU = mybir.AluOpType
    ACT = mybir.ActivationFunctionType
    AX = mybir.AxisListType

    GRAPHS, P, D = x.shape
    HID = w1.shape[0]
    KD = D // P
    KH = HID // P
    PAIRS = GRAPHS // 2
    EPS_DEG = 1e-6
    EPS_LN = 1e-5
    TINY = 1.17549435e-38
    STAT = D + 2

    x_d = x.rearrange("(n g) p d -> n p g d", g=2)
    adj_d = adj.rearrange("(n g) p e -> n p g e", g=2)
    out_d = out.rearrange("(n g) p d -> n p g d", g=2)

    ctx = ExitStack()
    with ctx:
        def sb(name, shape, dt=fp32):
            return ctx.enter_context(nc.sbuf_tensor(name, shape, dt))

        def sem(name):
            return ctx.enter_context(nc.semaphore(name))

        ident = sb("ident", [P, P])
        ident_bf = sb("ident_bf", [P, P], bf16)
        ones_col = sb("ones_col", [P, 2])
        ones_bf = sb("ones_bf", [P, 2], bf16)
        hid_mean = sb("hid_mean", [P, P])
        minus_half = sb("minus_half", [P, 2])
        floors = sb("floors", [P, 4])
        w0_raw = sb("w0_raw", [P, D // P, 2 * D])
        w1_raw = sb("w1_raw", [P, KH, D])
        w2_raw = sb("w2_raw", [P, D // P, HID])
        wab = [sb(f"wab_{part}", [P, KD, 2 * D], fp32r) for part in ("high", "low")]
        w1t = [sb(f"w1t_{part}", [P, KD, HID], fp32r) for part in ("high", "low")]
        w2t = sb("w2t", [P, KH, D])
        w2g = sb("w2g", [P, KH, D + 2])
        w2c = [sb(f"w2c_{part}", [P, KH, D + 2], fp32r) for part in ("high", "low")]
        b1_col = sb("b1_col", [P, KH])
        gamma_col = sb("gamma_col", [P, KH])
        beta_col = sb("beta_col", [P, KH])
        beta_wide = sb("beta_wide", [P, KH, P])
        b2_rows = sb("b2_rows", [P, D])
        b2_half = sb("b2_half", [P, D])
        beta_w2 = sb("beta_w2", [P, D])
        x_sb = sb("x_sb", [P, 2, 2, D])
        adj_sb = sb("adj_sb", [P, 2, 2, P])
        hub_sb = sb("hub_sb", [P, 2, 2, P])
        sums = sb("sums", [P, 4])
        safe = sb("safe", [P, 4])
        recips = sb("recips", [P, 4])
        dn = sb("dn", [P, 2])
        picked = sb("picked", [P, 2, P])
        edges = sb("edges", [P, 2, P], bf16)
        adj_n = sb("adj_n", [P, 2, P])
        edges_dn = sb("edges_dn", [P, 2, P])
        adj_t = sb("adj_t", [P, 2, 2, P])
        edges_dn_t = sb("edges_dn_t", [P, 2, P])
        counts = sb("counts", [P, 2])
        be = sb("be", [P, 2])
        edges_be_t = sb("edges_be_t", [P, 2, P])
        g_sb = sb("g_sb", [P, 2, 2, P])
        x_t = [sb(f"x_t_{part}", [P, 2, KD, P], fp32r) for part in ("high", "low")]
        yb_sb = sb("yb_sb", [P, 2, D])
        pre1 = sb("pre1", [P, 2, D])
        stats1 = sb("stats1", [P, 2, 6])
        mv1 = sb("mv1", [P, 2, 2])
        veps1 = sb("veps1", [P, 2])
        rstd1 = sb("rstd1", [P, 2])
        x1 = sb("x1", [P, 2, D])
        x1_b2 = sb("x1_b2", [P, 2, 2, D])
        u_t = [sb(f"u_t_{part}", [P, KD, 2, P], fp32r) for part in ("high", "low")]
        h = sb("h", [P, KH, 2, P])
        h_split = [sb(f"h_{part}", [P, KH, 2, P], fp32r) for part in ("high", "low")]
        h_sq = sb("h_sq", [P, KH, 2, P])
        h_sq2 = sb("h_sq2", [P, KH // 2, 2, P])
        h_sq1 = sb("h_sq1", [P, 2, P])
        hsum = sb("hsum", [P, 2, 2])
        mean_sq = sb("mean_sq", [P, 2])
        var_h = sb("var_h", [P, 2])
        veps_h = sb("veps_h", [P, 2])
        rstd_h = sb("rstd_h", [P, 2])
        q_sb = sb("q_sb", [P, 2, D])
        pre2 = sb("pre2", [P, 2, 2, D])
        stats2 = sb("stats2", [P, 2, 6])
        mv2 = sb("mv2", [P, 2, 2])
        veps2 = sb("veps2", [P, 2])
        rstd2 = sb("rstd2", [P, 2, 2])
        shift2 = sb("shift2", [P, 2, 2])
        out_sb = sb("out_sb", [P, 2, 2, D])

        bank = [ctx.enter_context(nc.psum_tensor(f"bank{i}", [P, 512], fp32)) for i in range(8)]
        ps_adj_t = bank[0][:, 0:2 * P]
        ps_edn_t = bank[0][:, 2 * P:4 * P]
        ps_edges_t = bank[1][:, 0:P].bitcast(bf16)
        ps_counts = bank[1][:, P:P + 2]
        ps_g = bank[1][:, 2 * P:4 * P]
        ps_x_t = bank[2]
        ps_y = [bank[3], bank[4]]
        ps_u_t = bank[5]
        ps_f = bank[2]
        ps_z = [bank[6], bank[7]]
        ps_q = [bank[6], bank[7]]

        s_w_in = [sem(f"w{i}_in") for i in range(3)]
        s_vectors_in = sem("vectors_in")
        s_consts = sem("consts")
        s_rows = sem("rows_ready")
        s_w_ps = [sem(f"w{i}_turned") for i in range(3)]
        s_w_hi = [sem(f"w{i}_high_ready") for i in range(3)]
        s_w_lo = [sem(f"w{i}_low_ready") for i in range(3)]
        s_w2t = sem("w2t_ready")
        s_w2g = sem("w2g_ready")
        s_beta_ps = sem("beta_in_psum")
        s_mean_ps = sem("mean_in_psum")
        s_beta_w2 = sem("beta_w2_ready")
        s_centred = sem("w2_centred")
        s_x_in = [sem(f"x_in{i}") for i in range(2)]
        s_adj_in = [sem(f"adj_in{i}") for i in range(2)]
        s_stored = [sem(f"stored{i}") for i in range(2)]
        s_sums = sem("sums_ready")
        s_safe = sem("safe_ready")
        s_recips = sem("recips_ready")
        s_dn = sem("dn_ready")
        s_prep = sem("prep_ready")
        s_adj_ps = sem("adj_transposed")
        s_adj_t = sem("adj_t_ready")
        s_edn_t = sem("edges_dn_t_ready")
        s_counts = sem("counts_ready")
        s_be = sem("be_ready")
        s_ebe_t = sem("edges_be_t_ready")
        s_g_ps = sem("g_in_psum")
        s_g = sem("g_ready")
        s_x_ps = sem("x_transposed")
        s_x_hi = sem("x_t_high_ready")
        s_x_t = sem("x_t_ready")
        s_y_ps = sem("y_in_psum")
        s_yb = sem("yb_ready")
        s_p_ps = sem("p_in_psum")
        s_pre1 = sem("pre1_ready")
        s_stats1 = sem("stats1_ready")
        s_mv1 = sem("mv1_ready")
        s_veps1 = sem("veps1_ready")
        s_rstd1 = sem("rstd1_ready")
        s_x1 = sem("x1_ready")
        s_x1_b2 = sem("x1_b2_ready")
        s_u_ps = sem("u_in_psum")
        s_u_hi = sem("u_t_high_ready")
        s_u_t = sem("u_t_ready")
        s_z_ps = sem("z_in_psum")
        s_h = sem("h_ready")
        s_h_hi = sem("h_high_ready")
        s_h_lo = sem("h_low_ready")
        s_h_sq = sem("h_sq_ready")
        s_h_sq2 = sem("h_sq2_ready")
        s_h_sq1 = sem("h_sq1_ready")
        s_q_ps = sem("q_in_psum")
        s_hsum = sem("hsum_ready")
        s_mean_sq = sem("mean_sq_ready")
        s_var_h = sem("var_h_ready")
        s_veps_h = sem("veps_h_ready")
        s_rstd_h = sem("rstd_h_ready")
        s_q = sem("q_ready")
        s_f_ps = sem("f_in_psum")
        s_pre2 = sem("pre2_ready")
        s_stats2 = sem("stats2_ready")
        s_mv2 = sem("mv2_ready")
        s_veps2 = sem("veps2_ready")
        s_rstd2 = sem("rstd2_ready")
        s_shift2 = sem("shift2_ready")
        s_out = sem("out_ready")

        HIGH, LOW = 0, 1
        PASSES = ((HIGH, HIGH), (HIGH, LOW), (LOW, HIGH))

        H_FIRST = [(HIGH, 0), (HIGH, 1), (LOW, 0), (LOW, 1), (HIGH, 2), (HIGH, 3)]
        H_LAST = [(LOW, 2), (LOW, 3)]

        def nth(i, c, per=1, k=0):
            return 2 * per * i + (per * c + k + 1)

        def loads(i, c):
            return 16 * i + 16 * (c // 2 + 1)

        def run(eng, step):
            for t in range(4):
                step(0, t)
            with eng.Fori(2, PAIRS // 2 - 2) as i:
                step(i, 0)
                step(i, 1)
            for t in range(PAIRS - 4, PAIRS + 3):
                step(0, t)

        def is_step(i, c, t):
            return isinstance(i, int) and c == t

        def live(i, c):
            return not isinstance(i, int) or 0 <= c < PAIRS

        def later(i, c, least):
            return not isinstance(i, int) or c >= least

        block = ctx.enter_context(nc.Block())

        @block.sync
        def _(sp):
            def load_adj(i, c):
                slot = c % 2
                if later(i, c, 2):
                    sp.wait_ge(s_prep, nth(i, c - 2, 3, 2))
                sp.dma_start(adj_sb[:, slot], adj_d[2 * i + c]).then_inc(s_adj_in[slot], 16)
                for g in range(2):
                    row = adj_d[2 * i + c, 0:1, g, :].to_broadcast([P, P])
                    sp.dma_start(hub_sb[:, slot, g], row).then_inc(s_adj_in[slot], 16)

            def load_x(i, c):
                slot = c % 2
                if later(i, c, 2):
                    sp.wait_ge(s_pre1, nth(i, c - 2, 2, 1))
                sp.dma_start(x_sb[:, slot], x_d[2 * i + c]).then_inc(s_x_in[slot], 16)

            load_x(0, 0)
            sp.dma_start(w0_raw[:, :, :], gnn_w.rearrange("(b p) f -> p b f", p=P)).then_inc(s_w_in[0], 16)
            load_adj(0, 0)
            sp.dma_start(w1_raw[:, :, :], w1.rearrange("(b p) f -> p b f", p=P)).then_inc(s_w_in[1], 16)
            load_x(0, 1)
            load_adj(0, 1)
            with nc.allow_non_contiguous_dma(reason="three vectors of 512, once"):
                for col, vec in ((b1_col, b1), (gamma_col, gamma), (beta_col, beta)):
                    sp.dma_start(col[:, :], vec.rearrange("(k p) -> p k", p=P)).then_inc(s_vectors_in, 16)
            sp.dma_start(b2_rows[:, :], b2.rearrange("(a d) -> a d", a=1).to_broadcast([P, D])).then_inc(s_vectors_in, 16)
            sp.dma_start(w2_raw[:, :, :], w2.rearrange("(b p) f -> p b f", p=P)).then_inc(s_w_in[2], 16)
            load_adj(0, 2)

            def step(i, c):
                if live(i, c + 3):
                    load_adj(i, c + 3)
                if live(i, c - 3):
                    sp.wait_ge(s_out, nth(i, c - 3, 2, 1))
                    sp.dma_start(out_d[2 * i + (c - 3)], out_sb[:, (c - 3) % 2]).then_inc(s_stored[(c - 3) % 2], 16)
                if live(i, c + 2):
                    load_x(i, c + 2)
            run(sp, step)
            for slot in range(2):
                sp.wait_ge(s_stored[slot], 16 * (PAIRS // 2))

        @block.gpsimd
        def _(pool):
            nc.gpsimd.memset(ident[:, :], 0.0).then_inc(s_consts, 1)
            nc.gpsimd.memset(ident_bf[:, :], 0.0).then_inc(s_consts, 1)
            nc.gpsimd.memset(ones_col[:, :], 1.0).then_inc(s_consts, 1)
            nc.gpsimd.memset(ones_bf[:, :], 1.0).then_inc(s_consts, 1)
            nc.gpsimd.memset(hid_mean[:, :], 1.0 / HID).then_inc(s_consts, 1)
            nc.gpsimd.memset(minus_half[:, :], -0.5).then_inc(s_consts, 1)
            nc.gpsimd.memset(floors[:, 0:2], EPS_DEG).then_inc(s_consts, 1)
            nc.gpsimd.memset(floors[:, 2:4], TINY).then_inc(s_consts, 1)
            nc.gpsimd.memset(w2g[:, :, D:D + 2], 1.0).then_inc(s_consts, 1)
            pool.wait_ge(s_consts, 9)
            for m in (ident, ident_bf):
                nc.gpsimd.affine_select(out=m[:, :], in_=m[:, :], compare_op=ALU.not_equal, fill=1.0,
                                        base=0, pattern=[[-1, P]], channel_multiplier=1).then_inc(s_consts, 1)
            pool.wait_ge(s_consts, 11)
            pool.wait_ge(s_rows, 1)

            def inverse_root(i, c, rstd, veps, s_veps, s_rstd):
                pool.wait_ge(s_veps, nth(i, c))
                nc.gpsimd.tensor_tensor(rstd, veps[:, :], minus_half[:, :], ALU.pow).then_inc(s_rstd, 1)

            def step(i, c):
                if live(i, c - 2):
                    inverse_root(i, c - 2, rstd_h[:, :], veps_h, s_veps_h, s_rstd_h)
                if live(i, c - 3):
                    inverse_root(i, c - 3, rstd2[:, (c - 3) % 2], veps2, s_veps2, s_rstd2)
                if live(i, c):
                    inverse_root(i, c, rstd1[:, :], veps1, s_veps1, s_rstd1)
                if live(i, c - 1):
                    for b in range(2):
                        pool.wait_ge(s_h_sq, nth(i, c - 1, 2, b))
                        nc.gpsimd.tensor_tensor(h_sq2[:, b], h_sq[:, 2 * b], h_sq[:, 2 * b + 1], ALU.add)\
                            .then_inc(s_h_sq2, 1)
                    pool.wait_ge(s_h_sq2, nth(i, c - 1, 2, 1))
                    nc.gpsimd.tensor_tensor(h_sq1[:, :], h_sq2[:, 0], h_sq2[:, 1], ALU.add).then_inc(s_h_sq1, 1)
                if live(i, c):
                    pool.wait_ge(s_x1, nth(i, c, 2, 1))
                    if later(i, c, 2):
                        pool.wait_ge(s_pre2, nth(i, c - 2, 2, 1))
                    for g in range(2):
                        nc.gpsimd.tensor_tensor(x1_b2[:, c % 2, g], x1[:, g], b2_half[:, :], ALU.add)\
                            .then_inc(s_x1_b2, 1)
            run(pool, step)

        @block.scalar
        def _(act):
            def copy_adj_t(i, c):
                act.wait_ge(s_adj_ps, nth(i, c))
                nc.scalar.activation(adj_t[:, c % 2], ps_adj_t, ACT.Copy).then_inc(s_adj_t, 1)
                nc.scalar.activation(edges_dn_t[:, :], ps_edn_t, ACT.Copy).then_inc(s_edn_t, 1)

            def scale_w2():
                for j in range(2):
                    act.wait_ge(s_w_ps[2], j + 1)
                    nc.scalar.activation(w2t[:, 2 * j:2 * j + 2], bank[5 + j][:, :], ACT.Copy).then_inc(s_w2t, 1)
                act.wait_ge(s_w2t, 2)
                for k in range(KH):
                    nc.scalar.activation(w2g[:, k, 0:D], w2t[:, k, :], ACT.Copy, scale=gamma_col[:, k:k + 1])\
                        .then_inc(s_w2g, 1)

            def copy_x_t(i, c):
                act.wait_ge(s_x_ps, nth(i, c))
                nc.scalar.activation(x_t[HIGH][:, :], ps_x_t[:, :], ACT.Copy).then_inc(s_x_hi, 1)

            def high_parts(n, parts, banks):
                for k in range(KD):
                    act.wait_ge(s_w_ps[n], k + 1)
                    nc.scalar.activation(parts[HIGH][:, k], banks[k][:, :], ACT.Copy).then_inc(s_w_hi[n], 1)

            def step(i, c):
                if live(i, c - 1):
                    act.wait_ge(s_u_ps, nth(i, c - 1))
                    nc.scalar.activation(u_t[HIGH][:, :], ps_u_t[:, :], ACT.Copy).then_inc(s_u_hi, 1)
                if live(i, c):
                    for g in range(2):
                        act.wait_ge(s_y_ps, nth(i, c, 2, g))
                        nc.scalar.activation(yb_sb[:, g], ps_y[g][:, D:2 * D], ACT.Copy).then_inc(s_yb, 1)
                if is_step(i, c, 0):
                    scale_w2()
                if live(i, c):
                    act.wait_ge(s_g_ps, nth(i, c))
                    if later(i, c, 2):
                        act.wait_ge(s_f_ps, nth(i, c - 2))
                    nc.scalar.activation(g_sb[:, c % 2], ps_g, ACT.Copy).then_inc(s_g, 1)
                if live(i, c - 1):
                    for m in range(KH):
                        act.wait_ge(s_z_ps, nth(i, c - 1, KH, m | 1))
                        nc.scalar.activation(h[:, m], ps_z[m // 2][:, (m % 2) * 2 * P:(m % 2 + 1) * 2 * P],
                                             ACT.Relu, bias=b1_col[:, m:m + 1]).then_inc(s_h, 1)
                        if m % 2:
                            act.wait_ge(s_h, nth(i, c - 1, KH, m))
                            nc.scalar.activation(h_split[HIGH][:, m - 1:m + 1], h[:, m - 1:m + 1], ACT.Copy)\
                                .then_inc(s_h_hi, 1)
                    for b in range(2):
                        nc.scalar.activation(h_sq[:, 2 * b:2 * b + 2], h[:, 2 * b:2 * b + 2], ACT.Square)\
                            .then_inc(s_h_sq, 1)
                if live(i, c + 1):
                    copy_x_t(i, c + 1)
                    copy_adj_t(i, c + 1)
                if live(i, c - 3):
                    act.wait_ge(s_shift2, nth(i, c - 3))
                    if later(i, c - 3, 2):
                        act.wait_ge(s_stored[(c - 3) % 2], loads(i, c - 5))
                    for g in range(2):
                        nc.scalar.activation(out_sb[:, (c - 3) % 2, g], pre2[:, (c - 3) % 2, g], ACT.Identity,
                                             bias=shift2[:, (c - 3) % 2, g:g + 1],
                                             scale=rstd2[:, (c - 3) % 2, g:g + 1]).then_inc(s_out, 1)

            high_parts(0, wab, ps_y)
            copy_x_t(0, 0)
            copy_adj_t(0, 0)
            high_parts(1, w1t, ps_z)
            act.wait_ge(s_vectors_in, 16 * 4)
            run(act, step)

        @block.vector
        def _(dve):
            def low_part(parts, full, s_high, s_low, value):
                dve.wait_ge(s_high, value)
                nc.vector.tensor_tensor(parts[LOW][:, :], full, parts[HIGH][:, :].bitcast(fp32), ALU.subtract)\
                    .then_inc(s_low, 1)

            def low_parts(n, parts, banks):
                for k in range(KD):
                    dve.wait_ge(s_w_hi[n], k + 1)
                    nc.vector.tensor_tensor(parts[LOW][:, k], banks[k][:, :], parts[HIGH][:, k].bitcast(fp32),
                                            ALU.subtract).then_inc(s_w_lo[n], 1)

            def centre_w2():
                dve.wait_ge(s_beta_ps, 1)
                nc.vector.tensor_copy(beta_w2[:, :], bank[7][:, 0:D]).then_inc(s_beta_w2, 1)
                dve.wait_ge(s_mean_ps, 1)
                nc.vector.tensor_tensor(w2g[:, :, 0:D], w2g[:, :, 0:D],
                                        bank[6][:, 0:D].unsqueeze(1).to_broadcast([P, KH, D]), ALU.subtract)\
                    .then_inc(s_centred, 1)
                dve.wait_ge(s_centred, 1)
                dve.wait_ge(s_consts, 11)
                nc.vector.tensor_copy(w2c[HIGH][:, :], w2g[:, :]).then_inc(s_w_hi[2], 1)
                low_part(w2c, w2g[:, :], s_w_hi[2], s_w_lo[2], 1)

            def prepare(i, c):
                slot = c % 2
                a = adj_sb[:, slot]
                dve.wait_ge(s_adj_in[slot], 3 * loads(i, c))
                nc.vector.tensor_reduce(sums[:, 0:2], a, AX.X, ALU.add).then_inc(s_sums, 1)
                for g in range(2):
                    nc.vector.scalar_tensor_tensor(
                        out=picked[:, g], in0=adj_sb[:, slot, g], scalar=0.0, in1=hub_sb[:, slot, g],
                        op0=ALU.not_equal, op1=ALU.mult, accum_out=sums[:, 2 + g:3 + g]).then_inc(s_sums, 1)
                if later(i, c, 1):
                    dve.wait_ge(s_adj_ps, nth(i, c - 1))
                nc.vector.tensor_scalar(edges[:, :], a, 0.0, None, ALU.not_equal).then_inc(s_prep, 1)
                dve.wait_ge(s_sums, nth(i, c, 3, 2))
                nc.vector.tensor_tensor(safe[:, :], sums[:, :], floors[:, :], ALU.max).then_inc(s_safe, 1)
                dve.wait_ge(s_safe, nth(i, c))
                nc.vector.reciprocal(recips[:, :], safe[:, :]).then_inc(s_recips, 1)
                dve.wait_ge(s_recips, nth(i, c))
                nc.vector.scalar_tensor_tensor(out=dn[:, :], in0=sums[:, 2:4], scalar=0.0, in1=recips[:, 2:4],
                                               op0=ALU.is_gt, op1=ALU.mult).then_inc(s_dn, 1)
                nc.vector.tensor_tensor(adj_n[:, :], a, recips[:, 0:2].unsqueeze(2).to_broadcast([P, 2, P]),
                                        ALU.mult).then_inc(s_prep, 1)
                dve.wait_ge(s_dn, nth(i, c))
                nc.vector.tensor_tensor(edges_dn[:, :], edges[:, :], dn[:, :].unsqueeze(2).to_broadcast([P, 2, P]),
                                        ALU.mult).then_inc(s_prep, 1)

            def invert_counts(i, c):
                dve.wait_ge(s_adj_ps, nth(i, c))
                nc.vector.tensor_scalar(counts[:, :], ps_counts, 1.0, None, ALU.max).then_inc(s_counts, 1)
                dve.wait_ge(s_counts, nth(i, c))
                nc.vector.reciprocal(be[:, :], counts[:, :]).then_inc(s_be, 1)

            def scale_edges(i, c):
                dve.wait_ge(s_be, nth(i, c))
                nc.vector.tensor_tensor(edges_be_t[:, :], ps_edges_t.rearrange("p (g e) -> p g e", g=2),
                                        be[:, :].unsqueeze(2).to_broadcast([P, 2, P]), ALU.mult)\
                    .then_inc(s_ebe_t, 1)

            def gather(i, c, pre, stats, s_pre, s_stats):
                for g in range(2):
                    dve.wait_ge(s_pre, nth(i, c, 2, g))
                    nc.vector.bn_stats(stats[:, g], pre[:, g]).then_inc(s_stats, 1)
                dve.wait_ge(s_stats, nth(i, c, 2, 1))

            def merge(i, c, stats, mv, veps, s_mv, s_veps):
                for g in range(2):
                    nc.vector.bn_aggr(mv[:, g], stats[:, g]).then_inc(s_mv, 1)
                dve.wait_ge(s_mv, nth(i, c, 2, 1))
                nc.vector.tensor_scalar(veps[:, :], mv[:, :, 1], EPS_LN, None, ALU.add).then_inc(s_veps, 1)

            def low_h(i, c, b):
                dve.wait_ge(s_h_hi, nth(i, c, 2, b))
                part = slice(2 * b, 2 * b + 2)
                nc.vector.tensor_tensor(h_split[LOW][:, part], h[:, part], h_split[HIGH][:, part].bitcast(fp32),
                                        ALU.subtract).then_inc(s_h_lo, 1)

            def step(i, c):
                if live(i, c - 1):
                    low_part(u_t, ps_u_t[:, :], s_u_hi, s_u_t, nth(i, c - 1))
                if live(i, c - 2):
                    dve.wait_ge(s_rstd_h, nth(i, c - 2))
                    for g in range(2):
                        nc.vector.scalar_tensor_tensor(
                            out=q_sb[:, g], in0=ps_q[g][:, 0:D], scalar=rstd_h[:, g:g + 1], in1=beta_w2[:, :],
                            op0=ALU.mult, op1=ALU.add).then_inc(s_q, 1)
                if live(i, c - 3):
                    merge(i, c - 3, stats2, mv2, veps2, s_mv2, s_veps2)
                if is_step(i, c, 0):
                    low_parts(1, w1t, ps_z)
                if live(i, c + 1):
                    prepare(i, c + 1)
                if live(i, c - 3):
                    dve.wait_ge(s_rstd2, nth(i, c - 3))
                    nc.vector.scalar_tensor_tensor(out=shift2[:, (c - 3) % 2], in0=mv2[:, :, 0], scalar=-1.0,
                                                   in1=rstd2[:, (c - 3) % 2],
                                                   op0=ALU.mult, op1=ALU.mult).then_inc(s_shift2, 1)
                if live(i, c):
                    dve.wait_ge(s_x_in[c % 2], loads(i, c))
                    for g in range(2):
                        dve.wait_ge(s_p_ps, nth(i, c, 2, g))
                        nc.vector.scalar_tensor_tensor(
                            out=pre1[:, g], in0=ps_y[g][:, 0:D], scalar=0.0, in1=x_sb[:, c % 2, g],
                            op0=ALU.max, op1=ALU.add).then_inc(s_pre1, 1)
                if live(i, c - 2):
                    dve.wait_ge(s_x1_b2, nth(i, c - 2, 2, 1))
                    dve.wait_ge(s_f_ps, nth(i, c - 2))
                    if later(i, c - 2, 2):
                        dve.wait_ge(s_out, nth(i, c - 4, 2, 1))
                    for g in range(2):
                        nc.vector.scalar_tensor_tensor(
                            out=pre2[:, c % 2, g], in0=x1_b2[:, c % 2, g], scalar=2.0, in1=ps_f[:, g * D:(g + 1) * D],
                            op0=ALU.mult, op1=ALU.add).then_inc(s_pre2, 1)
                if live(i, c):
                    gather(i, c, pre1, stats1, s_pre1, s_stats1)
                if live(i, c - 1):
                    low_h(i, c - 1, 0)
                if live(i, c):
                    merge(i, c, stats1, mv1, veps1, s_mv1, s_veps1)
                if live(i, c - 1):
                    low_h(i, c - 1, 1)
                if live(i, c):
                    dve.wait_ge(s_rstd1, nth(i, c))
                    if later(i, c, 1):
                        dve.wait_ge(s_x1_b2, nth(i, c - 1, 2, 1))
                    for g in range(2):
                        nc.vector.tensor_scalar(x1[:, g], pre1[:, g], mv1[:, g, 0:1], rstd1[:, g:g + 1],
                                                ALU.subtract, ALU.mult).then_inc(s_x1, 1)
                if live(i, c + 1):
                    low_part(x_t, ps_x_t[:, :], s_x_hi, s_x_t, nth(i, c + 1))
                if live(i, c - 2):
                    gather(i, c - 2, pre2[:, c % 2], stats2, s_pre2, s_stats2)
                if live(i, c + 1):
                    invert_counts(i, c + 1)
                if live(i, c - 1):
                    dve.wait_ge(s_q_ps, nth(i, c - 1))
                    for g in range(2):
                        nc.vector.tensor_copy(hsum[:, g], ps_q[g][:, D:D + 3:2]).then_inc(s_hsum, 1)
                    dve.wait_ge(s_hsum, nth(i, c - 1, 2, 1))
                    nc.vector.scalar_tensor_tensor(out=mean_sq[:, :], in0=hsum[:, :, 0], scalar=1.0 / HID ** 2,
                                                   in1=hsum[:, :, 0], op0=ALU.mult, op1=ALU.mult).then_inc(s_mean_sq, 1)
                if live(i, c + 1):
                    scale_edges(i, c + 1)
                if live(i, c - 1):
                    dve.wait_ge(s_mean_sq, nth(i, c - 1))
                    nc.vector.scalar_tensor_tensor(out=var_h[:, :], in0=hsum[:, :, 1], scalar=1.0 / HID,
                                                   in1=mean_sq[:, :], op0=ALU.mult, op1=ALU.subtract).then_inc(s_var_h, 1)
                    dve.wait_ge(s_var_h, nth(i, c - 1))
                    nc.vector.tensor_scalar(veps_h[:, :], var_h[:, :], 0.0, EPS_LN, ALU.max, ALU.add).then_inc(s_veps_h, 1)
                if is_step(i, c, 0):
                    centre_w2()

            dve.wait_ge(s_consts, 11)
            prepare(0, 0)
            low_parts(0, wab, ps_y)
            low_part(x_t, ps_x_t[:, :], s_x_hi, s_x_t, 1)
            invert_counts(0, 0)
            scale_edges(0, 0)
            dve.wait_ge(s_vectors_in, 16 * 4)
            nc.vector.tensor_scalar(b2_half[:, :], b2_rows[:, :], 0.5, None, ALU.mult).then_inc(s_rows, 1)
            nc.vector.tensor_copy(beta_wide[:, :, :], beta_col[:, :].unsqueeze(2).to_broadcast([P, KH, P]))\
                .then_inc(s_rows, 1)
            run(dve, step)

        @block.tensor
        def _(pe):
            mm = nc.tensor.matmul
            pe.wait_ge(s_consts, 11)

            def turn_weights(n, jobs):
                pe.wait_ge(s_w_in[n], 16)
                for dst, blocks in jobs:
                    for b, src in enumerate(blocks):
                        last = nc.tensor.transpose(dst[:, b * P:(b + 1) * P], src, ident[:, :])
                    last.then_inc(s_w_ps[n], 1)

            def turn_w0():
                turn_weights(0, [(ps_y[k], [w0_raw[:, b, f * D + k * P:f * D + (k + 1) * P]
                                            for f in range(2) for b in range(D // P)]) for k in range(KD)])

            def turn_w1():
                turn_weights(1, [(ps_z[k], [w1_raw[:, b, k * P:(k + 1) * P] for b in range(KH)]) for k in range(KD)])

            def turn_w2():
                pe.wait_ge(s_w_lo[1], KD)
                turn_weights(2, [(bank[5 + j], [w2_raw[:, b, k * P:(k + 1) * P] for k in (2 * j, 2 * j + 1)
                                            for b in range(D // P)]) for j in range(2)])

            def reduce_w2():
                pe.wait_ge(s_rows, 2)
                pe.wait_ge(s_w2g, KH)
                for k in range(KH):
                    last = mm(bank[7][:, 0:D], beta_wide[:, k, :], w2t[:, k, :], start=(k == 0), stop=(k == KH - 1))
                last.then_inc(s_beta_ps, 1)
                for k in range(KH):
                    last = mm(bank[6][:, 0:D], hid_mean[:, :], w2g[:, k, 0:D], start=(k == 0), stop=(k == KH - 1))
                last.then_inc(s_mean_ps, 1)

            def turn_x(i, c):
                slot = c % 2
                pe.wait_ge(s_x_in[slot], loads(i, c))
                if later(i, c, 1):
                    pe.wait_ge(s_x_t, nth(i, c - 1))
                if later(i, c, 3):
                    pe.wait_ge(s_pre2, nth(i, c - 3, 2, 1))
                for g in range(2):
                    for k in range(KD):
                        last = nc.tensor.transpose(ps_x_t[:, (g * KD + k) * P:(g * KD + k + 1) * P],
                                                   x_sb[:, slot, g, k * P:(k + 1) * P], ident[:, :])
                last.then_inc(s_x_ps, 1)

            def turn_adj(i, c):
                pe.wait_ge(s_prep, nth(i, c, 3, 2))
                if later(i, c, 1):
                    pe.wait_ge(s_adj_t, nth(i, c - 1))
                    pe.wait_ge(s_edn_t, nth(i, c - 1))
                    pe.wait_ge(s_g, nth(i, c - 1))
                for g in range(2):
                    nc.tensor.transpose(ps_adj_t[:, g * P:(g + 1) * P], adj_n[:, g], ident[:, :])
                    nc.tensor.transpose(ps_edn_t[:, g * P:(g + 1) * P], edges_dn[:, g], ident[:, :])
                    nc.tensor.transpose(ps_edges_t[:, g * P:(g + 1) * P], edges[:, g], ident_bf[:, :])
                    last = mm(ps_counts[:, g:g + 1], edges[:, g], ones_bf[:, 0:1], start=True, stop=True)
                last.then_inc(s_adj_ps, 1)

            def product(dst, blocks, left, right):
                for n, (a, b) in enumerate(PASSES):
                    for k in range(blocks):
                        last = mm(dst, left(a, k), right(b, k), start=(n == 0 and k == 0),
                                  stop=(n == len(PASSES) - 1 and k == blocks - 1))
                return last

            def step(i, c):
                if live(i, c):
                    pe.wait_ge(s_x_t, nth(i, c))
                    for g in range(2):
                        if later(i, c, 1):
                            pe.wait_ge(s_pre1, nth(i, c - 1, 2, g))
                        last = product(ps_y[g][:, :], KD, lambda a, k: x_t[a][:, g, k, :], lambda b, k: wab[b][:, k, :])
                        last.then_inc(s_y_ps, 1)
                if is_step(i, c, 0):
                    turn_w2()
                if live(i, c):
                    pe.wait_ge(s_ebe_t, nth(i, c))
                    pe.wait_ge(s_edn_t, nth(i, c))
                    for g in range(2):
                        last = mm(ps_g[:, g * P:(g + 1) * P], edges_be_t[:, g, :], edges_dn_t[:, g, :],
                                  start=True, stop=True)
                    last.then_inc(s_g_ps, 1)
                if live(i, c - 2):
                    for g in range(2):
                        pe.wait_ge(s_q, nth(i, c - 2, 2, g))
                        last = mm(ps_f[:, g * D:(g + 1) * D], g_sb[:, c % 2, g, :], q_sb[:, g, :],
                                  start=True, stop=True)
                    last.then_inc(s_f_ps, 1)
                if live(i, c):
                    pe.wait_ge(s_adj_t, nth(i, c))
                    for g in range(2):
                        pe.wait_ge(s_yb, nth(i, c, 2, g))
                        mm(ps_y[g][:, 0:D], adj_t[:, c % 2, g, :], yb_sb[:, g, :], start=False, stop=True,
                           skip_group_check=True)\
                            .then_inc(s_p_ps, 1)
                if live(i, c - 1):
                    if is_step(i, c, 1):
                        pe.wait_ge(s_beta_w2, 1)
                        pe.wait_ge(s_centred, 1)
                    pe.wait_ge(s_u_t, nth(i, c - 1))
                    if later(i, c - 1, 1):
                        pe.wait_ge(s_q, nth(i, c - 2, 2, 1))
                    for m in range(KH):
                        last = product(ps_z[m // 2][:, (m % 2) * 2 * P:(m % 2 + 1) * 2 * P], KD,
                                       lambda a, k: w1t[a][:, k, m * P:(m + 1) * P], lambda b, k: u_t[b][:, k])
                        last.then_inc(s_z_ps, 1)
                if live(i, c + 1):
                    turn_x(i, c + 1)
                    turn_adj(i, c + 1)
                if is_step(i, c, 0):
                    reduce_w2()
                if live(i, c - 1):
                    if is_step(i, c, 1):
                        pe.wait_ge(s_w_lo[2], 1)
                    for order in (H_FIRST, H_LAST):
                        for g in range(2):
                            for part, m in order:
                                if g == 0 and m % 2 == 0:
                                    pe.wait_ge((s_h_hi, s_h_lo)[part], nth(i, c - 1, 2, m // 2))
                                for other in ((HIGH, LOW) if part == HIGH else (HIGH,)):
                                    mm(ps_q[g][:, 0:D + 2], h_split[part][:, m, g, :], w2c[other][:, m, :],
                                       start=((part, m, other) == (HIGH, 0, HIGH)), stop=((part, m) == H_LAST[-1]))
                if live(i, c):
                    pe.wait_ge(s_g, nth(i, c))
                    for g in range(2):
                        pe.wait_ge(s_x1, nth(i, c, 2, g))
                        for k in range(KD):
                            last = mm(ps_u_t[:, (k * 2 + g) * P:(k * 2 + g + 1) * P], x1[:, g, k * P:(k + 1) * P],
                                      g_sb[:, c % 2, g, :], start=True, stop=True)
                    last.then_inc(s_u_ps, 1)
                if live(i, c - 1):
                    pe.wait_ge(s_h_sq1, nth(i, c - 1))
                    for g in range(2):
                        last = mm(ps_q[g][:, STAT:STAT + 1], h_sq1[:, g, :], ones_col[:, 0:1], start=True, stop=True)
                    last.then_inc(s_q_ps, 1)

            turn_w0()
            turn_x(0, 0)
            turn_adj(0, 0)
            turn_w1()
            pe.wait_ge(s_w_lo[0], KD)
            run(pe, step)


_INS = ['x', 'adj', 'L0_gnn_W', 'L1_gnn_W1', 'L1_gnn_b1', 'L1_gnn_gamma', 'L1_gnn_beta', 'L1_gnn_W2', 'L1_gnn_b2']
_OUTS = [((64, 128, 256), 'float32')]


def kernel(**inputs):
    import numpy as _np
    import concourse.bacc as _bacc
    from concourse import mybir as _mybir
    from concourse.bass_utils import run_bass_kernel_spmd as _run

    nc = _bacc.Bacc("TRN2", target_bir_lowering=False, num_devices=1)
    arrays, args = {}, []
    for name in _INS:
        a = _np.ascontiguousarray(inputs[name])
        arrays[f"in_{name}_dram"] = a
        args.append(nc.dram_tensor(f"in_{name}_dram", a.shape, _mybir.dt.from_np(a.dtype), kind="ExternalInput").ap())
    for i, (shape, dtype) in enumerate(_OUTS):
        dt = _mybir.dt.from_np(_np.dtype(dtype))
        args.append(nc.dram_tensor(f"out_{i}_dram", shape, dt, kind="ExternalOutput").ap())
    gnn_hypergraph_kernel(nc, *args)
    r = _run(nc, [arrays], core_ids=[0])
    got = tuple(r.results[0][f"out_{i}_dram"] for i in range(len(_OUTS)))
    return got[0]
```

```python
import concourse.bass as bass
from concourse import mybir
from contextlib import ExitStack


def gnn_hypergraph_kernel(nc: bass.Bass, x: bass.AP, adj: bass.AP, gnn_w: bass.AP, w1: bass.AP,
                          b1: bass.AP, gamma: bass.AP, beta: bass.AP, w2: bass.AP, b2: bass.AP,
                          out: bass.AP):
    fp32 = mybir.dt.float32
    fp32r = mybir.dt.float32r
    bf16 = mybir.dt.bfloat16
    ALU = mybir.AluOpType
    ACT = mybir.ActivationFunctionType
    AX = mybir.AxisListType

    GRAPHS, P, D = x.shape
    HID = w1.shape[0]
    KD = D // P
    KH = HID // P
    PAIRS = GRAPHS // 2
    EPS_DEG = 1e-6
    EPS_LN = 1e-5
    TINY = 1.17549435e-38
    STAT = D + 2

    x_d = x.rearrange("(n g) p d -> n p g d", g=2)
    adj_d = adj.rearrange("(n g) p e -> n p g e", g=2)
    out_d = out.rearrange("(n g) p d -> n p g d", g=2)

    ctx = ExitStack()
    with ctx:
        def sb(name, shape, dt=fp32):
            return ctx.enter_context(nc.sbuf_tensor(name, shape, dt))

        def sem(name):
            return ctx.enter_context(nc.semaphore(name))

        ident = sb("ident", [P, P])
        ident_ones = sb("ident_ones", [P, P + 2], bf16)
        ones_col = sb("ones_col", [P, 2])
        minus_half = sb("minus_half", [P, 2])
        floors = sb("floors", [P, 4])
        w0_raw = sb("w0_raw", [P, D // P, 2 * D])
        w1_raw = sb("w1_raw", [P, KH, D])
        w2_raw = sb("w2_raw", [P, D // P, HID])
        wab = [sb(f"wab_{part}", [P, KD, 2 * D], fp32r) for part in ("high", "low")]
        w1t = [sb(f"w1t_{part}", [P, KD, HID], fp32r) for part in ("high", "low")]
        w2t = sb("w2t", [P, KH, D])
        w2g = sb("w2g", [P, KH, D + 2])
        w2c = [sb(f"w2c_{part}", [P, KH, D + 2], fp32r) for part in ("high", "low")]
        b1_col = sb("b1_col", [P, KH])
        gamma_col = sb("gamma_col", [P, KH])
        beta_col = sb("beta_col", [P, KH])
        gamma_wide = sb("gamma_wide", [P, KH, P])
        beta_wide = sb("beta_wide", [P, KH, P])
        b2_rows = sb("b2_rows", [P, D])
        b2_half = sb("b2_half", [P, D])
        beta_w2 = sb("beta_w2", [P, D])
        x_sb = sb("x_sb", [P, 2, 2, D])
        adj_sb = sb("adj_sb", [P, 2, 2, P])
        hub_sb = sb("hub_sb", [P, 2, 2, P])
        sums = sb("sums", [P, 4])
        safe = sb("safe", [P, 4])
        recips = sb("recips", [P, 4])
        dn = sb("dn", [P, 2])
        picked = sb("picked", [P, 2, P])
        edges = sb("edges", [P, 2, P], bf16)
        adj_n = sb("adj_n", [P, 2, P])
        edges_dn = sb("edges_dn", [P, 2, P])
        adj_t = sb("adj_t", [P, 2, P])
        adj_t_split = [sb(f"adj_t_{part}", [P, 2, 2, P], fp32r) for part in ("high", "low")]
        edges_dn_t = sb("edges_dn_t", [P, 2, P])
        counts = sb("counts", [P, 2])
        be = sb("be", [P, 2])
        edges_be_t = sb("edges_be_t", [P, 2, P])
        g_sb = sb("g_sb", [P, 2, 2, P])
        g_split = [sb(f"g_{part}", [P, 2, 2, P], fp32r) for part in ("high", "low")]
        x_t = [sb(f"x_t_{part}", [P, 2, KD, P], fp32r) for part in ("high", "low")]
        yb = [sb(f"yb_{part}", [P, 2, D], fp32r) for part in ("high", "low")]
        pre1 = sb("pre1", [P, 2, D])
        stats1 = sb("stats1", [P, 2, 6])
        mv1 = sb("mv1", [P, 2, 2])
        veps1 = sb("veps1", [P, 2])
        rstd1 = sb("rstd1", [P, 2])
        x1 = sb("x1", [P, 2, D])
        x1_b2 = sb("x1_b2", [P, 2, 2, D])
        u_t = [sb(f"u_t_{part}", [P, KD, 2, P], fp32r) for part in ("high", "low")]
        h = sb("h", [P, KH, 2, P])
        h_split = [sb(f"h_{part}", [P, KH, 2, P], fp32r) for part in ("high", "low")]
        h_sq = sb("h_sq", [P, KH, 2, P])
        h_sq2 = sb("h_sq2", [P, KH // 2, 2, P])
        h_sq1 = sb("h_sq1", [P, 2, P])
        hsum = sb("hsum", [P, 2, 2])
        mean_sq = sb("mean_sq", [P, 2])
        var_h = sb("var_h", [P, 2])
        veps_h = sb("veps_h", [P, 2])
        rstd_h = sb("rstd_h", [P, 2])
        q_sb = sb("q_sb", [P, 2, D])
        q_split = [sb(f"q_{part}", [P, 2, D], fp32r) for part in ("high", "low")]
        pre2 = sb("pre2", [P, 2, 2, D])
        stats2 = sb("stats2", [P, 2, 6])
        mv2 = sb("mv2", [P, 2, 2])
        veps2 = sb("veps2", [P, 2])
        rstd2 = sb("rstd2", [P, 2, 2])
        shift2 = sb("shift2", [P, 2, 2])
        out_sb = sb("out_sb", [P, 2, 2, D])

        bank = [ctx.enter_context(nc.psum_tensor(f"bank{i}", [P, 512], fp32)) for i in range(8)]
        ps_adj_t = bank[0][:, 0:2 * P]
        ps_edn_t = bank[0][:, 2 * P:4 * P]
        ps_edges_t = bank[1][:, 0:2 * (P + 2)].rearrange("p (g e) -> p g e", g=2)
        ps_g = bank[5][:, 0:2 * P]
        ps_x_t = bank[2]
        ps_y = [bank[3], bank[4]]
        ps_u_t = bank[5]
        ps_f = [bank[3][:, D:2 * D], bank[4][:, D:2 * D]]
        ps_z = [bank[6], bank[7]]
        ps_z_last = [bank[0], bank[2]]
        ps_q = [bank[6], bank[7]]

        s_w_in = [sem(f"w{i}_in") for i in range(3)]
        s_vectors_in = sem("vectors_in")
        s_consts = sem("consts")
        s_wide = sem("wide_ready")
        s_b2_half = sem("b2_half_ready")
        s_w_ps = [sem(f"w{i}_turned") for i in range(3)]
        s_w_hi = [sem(f"w{i}_high_ready") for i in range(3)]
        s_w_lo = [sem(f"w{i}_low_ready") for i in range(3)]
        s_w2t = sem("w2t_ready")
        s_w2g = sem("w2g_ready")
        s_beta_ps = sem("beta_in_psum")
        s_sum_ps = sem("gamma_sum_in_psum")
        s_beta_w2 = sem("beta_w2_ready")
        s_centred = sem("w2_centred")
        s_x_in = [sem(f"x_in{i}") for i in range(2)]
        s_adj_in = [sem(f"adj_in{i}") for i in range(2)]
        s_stored = [sem(f"stored{i}") for i in range(2)]
        s_sums = sem("sums_ready")
        s_safe = sem("safe_ready")
        s_recips = sem("recips_ready")
        s_dn = sem("dn_ready")
        s_prep = sem("prep_ready")
        s_adj_ps = sem("adj_transposed")
        s_adj_n = sem("adj_n_ready")
        s_adj_t = sem("adj_t_ready")
        s_adj_hi = sem("adj_t_high_ready")
        s_adj_lo = sem("adj_t_low_ready")
        s_edn_t = sem("edges_dn_t_ready")
        s_counts = sem("counts_ready")
        s_be = sem("be_ready")
        s_ebe_t = sem("edges_be_t_ready")
        s_g_ps = sem("g_in_psum")
        s_g = sem("g_ready")
        s_g_hi = sem("g_high_ready")
        s_g_lo = sem("g_low_ready")
        s_x_ps = sem("x_transposed")
        s_x_hi = sem("x_t_high_ready")
        s_x_t = sem("x_t_ready")
        s_y_ps = sem("y_in_psum")
        s_yb_hi = sem("yb_high_ready")
        s_yb = sem("yb_ready")
        s_p_ps = sem("p_in_psum")
        s_pre1 = sem("pre1_ready")
        s_stats1 = sem("stats1_ready")
        s_mv1 = sem("mv1_ready")
        s_veps1 = sem("veps1_ready")
        s_rstd1 = sem("rstd1_ready")
        s_x1 = sem("x1_ready")
        s_x1_b2 = sem("x1_b2_ready")
        s_u_ps = sem("u_in_psum")
        s_u_hi = sem("u_t_high_ready")
        s_u_t = sem("u_t_ready")
        s_z_ps = sem("z_in_psum")
        s_h = sem("h_ready")
        s_h_hi = sem("h_high_ready")
        s_h_lo = sem("h_low_ready")
        s_h_sq = sem("h_sq_ready")
        s_h_sq2 = sem("h_sq2_ready")
        s_h_sq1 = sem("h_sq1_ready")
        s_q_ps = sem("q_in_psum")
        s_hsum = sem("hsum_ready")
        s_mean_sq = sem("mean_sq_ready")
        s_var_h = sem("var_h_ready")
        s_veps_h = sem("veps_h_ready")
        s_rstd_h = sem("rstd_h_ready")
        s_q = sem("q_ready")
        s_q_hi = sem("q_high_ready")
        s_q_lo = sem("q_low_ready")
        s_f_ps = sem("f_in_psum")
        s_pre2 = sem("pre2_ready")
        s_stats2 = sem("stats2_ready")
        s_mv2 = sem("mv2_ready")
        s_veps2 = sem("veps2_ready")
        s_rstd2 = sem("rstd2_ready")
        s_shift2 = sem("shift2_ready")
        s_out = sem("out_ready")

        CONSTS = 10
        HIGH, LOW = 0, 1
        PASSES = ((HIGH, HIGH), (HIGH, LOW), (LOW, HIGH))

        H_ORDER = [[(HIGH, 0), (HIGH, 1), (LOW, 0), (LOW, 1)], [(HIGH, 2), (HIGH, 3)], [(LOW, 2), (LOW, 3)]]

        UNROLL = 4

        def nth(i, c, per=1, k=0):
            return UNROLL * per * i + (per * c + k + 1)

        def loads(i, c):
            return UNROLL // 2 * 16 * i + 16 * (c // 2 + 1)

        def run(eng, step):
            for t in range(4):
                step(0, t)
            with eng.Fori(4 // UNROLL, (PAIRS - 4) // UNROLL) as i:
                for c in range(UNROLL):
                    step(i, c)
            for t in range(PAIRS - 4, PAIRS + 3):
                step(0, t)

        def is_step(i, c, t):
            return isinstance(i, int) and c == t

        def live(i, c):
            return not isinstance(i, int) or 0 <= c < PAIRS

        def is_drain(i, c):
            return isinstance(i, int) and c >= PAIRS

        def splits_q(i, c):
            return live(i, c) and not is_drain(i, c + 2)

        def is_last(i, c):
            return is_step(i, c, PAIRS - 1)

        def z_banks(i, c):
            return ps_z_last if is_last(i, c) else ps_z

        def later(i, c, least):
            return not isinstance(i, int) or c >= least

        def sum_squares(ops, eng, i, c):
            for b in range(2):
                eng.wait_ge(s_h_sq, nth(i, c, 2, b))
                ops.tensor_tensor(h_sq2[:, b], h_sq[:, 2 * b], h_sq[:, 2 * b + 1], ALU.add).then_inc(s_h_sq2, 1)
            eng.wait_ge(s_h_sq2, nth(i, c, 2, 1))
            ops.tensor_tensor(h_sq1[:, :], h_sq2[:, 0], h_sq2[:, 1], ALU.add).then_inc(s_h_sq1, 1)

        block = ctx.enter_context(nc.Block())

        @block.sync
        def _(sp):
            def load_adj(i, c):
                slot = c % 2
                if later(i, c, 2):
                    sp.wait_ge(s_prep, nth(i, c - 2, 2, 1))
                    sp.wait_ge(s_adj_n, nth(i, c - 2, 2, 1))
                sp.dma_start(adj_sb[:, slot], adj_d[UNROLL * i + c]).then_inc(s_adj_in[slot], 16)
                for g in range(2):
                    row = adj_d[UNROLL * i + c, 0:1, g, :].to_broadcast([P, P])
                    sp.dma_start(hub_sb[:, slot, g], row).then_inc(s_adj_in[slot], 16)

            def load_x(i, c):
                slot = c % 2
                if later(i, c, 2):
                    sp.wait_ge(s_pre1, nth(i, c - 2, 2, 1))
                sp.dma_start(x_sb[:, slot], x_d[UNROLL * i + c]).then_inc(s_x_in[slot], 16)

            load_x(0, 0)
            sp.dma_start(w0_raw[:, :, :], gnn_w.rearrange("(b p) f -> p b f", p=P)).then_inc(s_w_in[0], 16)
            load_adj(0, 0)
            sp.dma_start(w1_raw[:, :, :], w1.rearrange("(b p) f -> p b f", p=P)).then_inc(s_w_in[1], 16)
            load_x(0, 1)
            load_adj(0, 1)
            with nc.allow_non_contiguous_dma(reason="three vectors of 512, once"):
                for col, vec in ((b1_col, b1), (gamma_col, gamma), (beta_col, beta)):
                    sp.dma_start(col[:, :], vec.rearrange("(k p) -> p k", p=P)).then_inc(s_vectors_in, 16)
            sp.dma_start(b2_rows[:, :], b2.rearrange("(a d) -> a d", a=1).to_broadcast([P, D])).then_inc(s_vectors_in, 16)
            sp.dma_start(w2_raw[:, :, :], w2.rearrange("(b p) f -> p b f", p=P)).then_inc(s_w_in[2], 16)
            load_adj(0, 2)

            def step(i, c):
                if live(i, c + 3):
                    load_adj(i, c + 3)
                if live(i, c + 2):
                    load_x(i, c + 2)
                if live(i, c - 3):
                    sp.wait_ge(s_out, nth(i, c - 3, 2, 1))
                    sp.dma_start(out_d[UNROLL * i + (c - 3)], out_sb[:, (c - 3) % 2]).then_inc(s_stored[(c - 3) % 2], 16)
            run(sp, step)
            for slot in range(2):
                sp.wait_ge(s_stored[slot], 16 * (PAIRS // 2))

        @block.gpsimd
        def _(pool):
            nc.gpsimd.memset(ident[:, :], 0.0).then_inc(s_consts, 1)
            nc.gpsimd.memset(ident_ones[:, 0:P], 0.0).then_inc(s_consts, 1)
            nc.gpsimd.memset(ones_col[:, :], 1.0).then_inc(s_consts, 1)
            nc.gpsimd.memset(ident_ones[:, P:P + 2], 1.0).then_inc(s_consts, 1)
            nc.gpsimd.memset(minus_half[:, :], -0.5).then_inc(s_consts, 1)
            nc.gpsimd.memset(floors[:, 0:2], EPS_DEG).then_inc(s_consts, 1)
            nc.gpsimd.memset(floors[:, 2:4], TINY).then_inc(s_consts, 1)
            nc.gpsimd.memset(w2g[:, :, D:D + 2], 1.0).then_inc(s_consts, 1)
            pool.wait_ge(s_consts, 8)
            for m in (ident, ident_ones):
                nc.gpsimd.affine_select(out=m[:, 0:P], in_=m[:, 0:P], compare_op=ALU.not_equal, fill=1.0,
                                        base=0, pattern=[[-1, P]], channel_multiplier=1).then_inc(s_consts, 1)
            pool.wait_ge(s_consts, CONSTS)

            def inverse_root(i, c, rstd, veps, s_veps, s_rstd):
                pool.wait_ge(s_veps, nth(i, c))
                nc.gpsimd.tensor_tensor(rstd, veps[:, :], minus_half[:, :], ALU.pow).then_inc(s_rstd, 1)

            def low_part(low, full, high, s_low):
                nc.gpsimd.tensor_tensor(low, full, high.bitcast(fp32), ALU.subtract).then_inc(s_low, 1)

            def widen(wide, col):
                nc.gpsimd.tensor_copy(wide[:, :, :], col[:, :].unsqueeze(2).to_broadcast([P, KH, P])).then_inc(s_wide, 1)

            def step(i, c):
                if live(i, c):
                    pool.wait_ge(s_adj_t, nth(i, c))
                    pool.wait_ge(s_adj_hi, nth(i, c))
                    slot = c % 2
                    low_part(adj_t_split[LOW][:, slot], adj_t[:, :], adj_t_split[HIGH][:, slot], s_adj_lo)
                if is_step(i, c, 0):
                    widen(gamma_wide, gamma_col)
                if live(i, c - 2):
                    inverse_root(i, c - 2, rstd_h[:, :], veps_h, s_veps_h, s_rstd_h)
                if splits_q(i, c - 2):
                    if later(i, c - 2, 1):
                        pool.wait_ge(s_f_ps, nth(i, c - 3, 2, 1))
                    for g in range(2):
                        pool.wait_ge(s_q_hi, nth(i, c - 2, 2, g))
                        low_part(q_split[LOW][:, g], q_sb[:, g], q_split[HIGH][:, g], s_q_lo)
                if is_step(i, c, 1):
                    pool.wait_ge(s_w_hi[2], 1)
                    low_part(w2c[LOW][:, :], w2g[:, :], w2c[HIGH][:, :], s_w_lo[2])
                if live(i, c - 3):
                    inverse_root(i, c - 3, rstd2[:, (c - 3) % 2], veps2, s_veps2, s_rstd2)
                if splits_q(i, c - 1):
                    pool.wait_ge(s_g_hi, nth(i, c - 1))
                    slot = (c - 1) % 2
                    low_part(g_split[LOW][:, slot], g_sb[:, slot], g_split[HIGH][:, slot], s_g_lo)
                if live(i, c):
                    inverse_root(i, c, rstd1[:, :], veps1, s_veps1, s_rstd1)
                if live(i, c - 1) and not is_last(i, c - 1):
                    sum_squares(nc.gpsimd, pool, i, c - 1)
                if live(i, c):
                    if is_step(i, c, 0):
                        pool.wait_ge(s_b2_half, 1)
                    pool.wait_ge(s_x1, nth(i, c, 2, 1))
                    if later(i, c, 2):
                        pool.wait_ge(s_pre2, nth(i, c - 2, 2, 1))
                    for g in range(2):
                        nc.gpsimd.tensor_tensor(x1_b2[:, c % 2, g], x1[:, g], b2_half[:, :], ALU.add)\
                            .then_inc(s_x1_b2, 1)
            pool.wait_ge(s_vectors_in, 16 * 4)
            widen(beta_wide, beta_col)
            run(pool, step)

        @block.scalar
        def _(act):
            def copy_adj_t(i, c):
                act.wait_ge(s_adj_ps, nth(i, c))
                if later(i, c, 1):
                    act.wait_ge(s_adj_lo, nth(i, c - 1))
                nc.scalar.activation(adj_t[:, :], ps_adj_t, ACT.Copy).then_inc(s_adj_t, 1)
                nc.scalar.activation(adj_t_split[HIGH][:, c % 2], ps_adj_t, ACT.Copy).then_inc(s_adj_hi, 1)
                nc.scalar.activation(edges_dn_t[:, :], ps_edn_t, ACT.Copy).then_inc(s_edn_t, 1)

            def scale_adj(i, c):
                act.wait_ge(s_recips, nth(i, c))
                for g in range(2):
                    nc.scalar.activation(adj_n[:, g], adj_sb[:, c % 2, g], ACT.Copy, scale=recips[:, g:g + 1])\
                        .then_inc(s_adj_n, 1)

            def scale_edges(i, c):
                act.wait_ge(s_be, nth(i, c))
                for g in range(2):
                    nc.scalar.activation(edges_be_t[:, g], ps_edges_t[:, g, 0:P], ACT.Copy, scale=be[:, g:g + 1])\
                        .then_inc(s_ebe_t, 1)

            def relu_h(i, c, b):
                act.wait_ge(s_z_ps, nth(i, c, KH, 2 * b + 1))
                for m in (2 * b, 2 * b + 1):
                    nc.scalar.activation(h[:, m], z_banks(i, c)[b][:, (m % 2) * 2 * P:(m % 2 + 1) * 2 * P],
                                         ACT.Relu, bias=b1_col[:, m:m + 1]).then_inc(s_h, 1)
                act.wait_ge(s_h, nth(i, c, KH, 2 * b + 1))
                part = slice(2 * b, 2 * b + 2)
                nc.scalar.activation(h_split[HIGH][:, part], h[:, part], ACT.Copy).then_inc(s_h_hi, 1)

            def square_h(b):
                part = slice(2 * b, 2 * b + 2)
                nc.scalar.activation(h_sq[:, part], h[:, part], ACT.Square).then_inc(s_h_sq, 1)

            def copy_w2():
                for j in range(2):
                    act.wait_ge(s_w_ps[2], j + 1)
                    nc.scalar.activation(w2t[:, 2 * j:2 * j + 2], bank[6 + j][:, :], ACT.Copy).then_inc(s_w2t, 1)

            def scale_w2():
                act.wait_ge(s_w2t, 2)
                for k in range(KH):
                    nc.scalar.activation(w2g[:, k, 0:D], w2t[:, k, :], ACT.Copy, scale=gamma_col[:, k:k + 1])\
                        .then_inc(s_w2g, 1)

            def copy_x_t(i, c):
                act.wait_ge(s_x_ps, nth(i, c))
                nc.scalar.activation(x_t[HIGH][:, :], ps_x_t[:, :], ACT.Copy).then_inc(s_x_hi, 1)

            def high_parts(n, parts, banks):
                for k in range(KD):
                    act.wait_ge(s_w_ps[n], k + 1)
                    nc.scalar.activation(parts[HIGH][:, k], banks[k][:, :], ACT.Copy).then_inc(s_w_hi[n], 1)

            def step(i, c):
                if splits_q(i, c - 1):
                    if later(i, c - 1, 2):
                        act.wait_ge(s_f_ps, nth(i, c - 3, 2, 1))
                    slot = (c - 1) % 2
                    nc.scalar.activation(g_split[HIGH][:, slot], g_sb[:, slot], ACT.Copy).then_inc(s_g_hi, 1)
                if live(i, c):
                    for g in range(2):
                        act.wait_ge(s_y_ps, nth(i, c, 2, g))
                        nc.scalar.activation(yb[HIGH][:, g], ps_y[g][:, D:2 * D], ACT.Copy).then_inc(s_yb_hi, 1)
                if is_step(i, c, 0):
                    copy_adj_t(0, 0)
                    scale_edges(0, 0)
                    copy_w2()
                if is_step(i, c, 1):
                    act.wait_ge(s_centred, 1)
                    nc.scalar.activation(w2c[HIGH][:, :], w2g[:, :], ACT.Copy).then_inc(s_w_hi[2], 1)
                if splits_q(i, c - 2):
                    if later(i, c - 2, 1):
                        act.wait_ge(s_f_ps, nth(i, c - 3, 2, 1))
                    for g in range(2):
                        act.wait_ge(s_q, nth(i, c - 2, 2, g))
                        nc.scalar.activation(q_split[HIGH][:, g], q_sb[:, g], ACT.Copy).then_inc(s_q_hi, 1)
                if live(i, c):
                    act.wait_ge(s_g_ps, nth(i, c))
                    nc.scalar.activation(g_sb[:, c % 2], ps_g, ACT.Copy).then_inc(s_g, 1)
                if live(i, c + 1):
                    copy_x_t(i, c + 1)
                    scale_adj(i, c + 1)
                if is_step(i, c, 0):
                    scale_w2()
                if live(i, c - 1):
                    relu_h(i, c - 1, 0)
                    relu_h(i, c - 1, 1)
                    square_h(0)
                    square_h(1)
                if live(i, c + 1):
                    copy_adj_t(i, c + 1)
                    scale_edges(i, c + 1)
                if live(i, c):
                    act.wait_ge(s_u_ps, nth(i, c))
                    nc.scalar.activation(u_t[HIGH][:, :], ps_u_t[:, :], ACT.Copy).then_inc(s_u_hi, 1)
                if live(i, c - 3):
                    act.wait_ge(s_shift2, nth(i, c - 3))
                    if later(i, c - 3, 2):
                        act.wait_ge(s_stored[(c - 3) % 2], loads(i, c - 5))
                    for g in range(1 if is_last(i, c - 3) else 2):
                        nc.scalar.activation(out_sb[:, (c - 3) % 2, g], pre2[:, (c - 3) % 2, g], ACT.Identity,
                                             bias=shift2[:, (c - 3) % 2, g:g + 1],
                                             scale=rstd2[:, (c - 3) % 2, g:g + 1]).then_inc(s_out, 1)

            copy_x_t(0, 0)
            high_parts(0, wab, ps_y)
            high_parts(1, w1t, ps_z)
            scale_adj(0, 0)
            act.wait_ge(s_vectors_in, 16 * 4)
            run(act, step)

        @block.vector
        def _(dve):
            def low_part(parts, full, s_high, s_low, value):
                dve.wait_ge(s_high, value)
                nc.vector.tensor_tensor(parts[LOW][:, :], full, parts[HIGH][:, :].bitcast(fp32), ALU.subtract)\
                    .then_inc(s_low, 1)

            def low_parts(n, parts, banks):
                for k in range(KD):
                    dve.wait_ge(s_w_hi[n], k + 1)
                    nc.vector.tensor_tensor(parts[LOW][:, k], banks[k][:, :], parts[HIGH][:, k].bitcast(fp32),
                                            ALU.subtract).then_inc(s_w_lo[n], 1)

            def centre_w2():
                dve.wait_ge(s_beta_ps, 1)
                nc.vector.tensor_copy(beta_w2[:, :], bank[7][:, 0:D]).then_inc(s_beta_w2, 1)
                dve.wait_ge(s_sum_ps, 1)
                dve.wait_ge(s_w2g, KH)
                nc.vector.scalar_tensor_tensor(
                    out=w2g[:, :, 0:D], in0=bank[6][:, 0:D].unsqueeze(1).to_broadcast([P, KH, D]), scalar=-1.0 / HID,
                    in1=w2g[:, :, 0:D], op0=ALU.mult, op1=ALU.add).then_inc(s_centred, 1)

            def sum_adj(i, c):
                slot = c % 2
                a = adj_sb[:, slot]
                dve.wait_ge(s_adj_in[slot], 3 * loads(i, c))
                nc.vector.tensor_reduce(sums[:, 0:2], a, AX.X, ALU.add).then_inc(s_sums, 1)
                for g in range(2):
                    nc.vector.scalar_tensor_tensor(
                        out=picked[:, g], in0=adj_sb[:, slot, g], scalar=0.0, in1=hub_sb[:, slot, g],
                        op0=ALU.not_equal, op1=ALU.mult, accum_out=sums[:, 2 + g:3 + g]).then_inc(s_sums, 1)
                if later(i, c, 1):
                    dve.wait_ge(s_adj_ps, nth(i, c - 1))
                nc.vector.tensor_scalar(edges[:, :], a, 0.0, None, ALU.not_equal).then_inc(s_prep, 1)

            def invert_sums(i, c):
                dve.wait_ge(s_sums, nth(i, c, 3, 2))
                nc.vector.tensor_tensor(safe[:, :], sums[:, :], floors[:, :], ALU.max).then_inc(s_safe, 1)
                dve.wait_ge(s_safe, nth(i, c))
                if later(i, c, 1):
                    dve.wait_ge(s_adj_n, nth(i, c - 1, 2, 1))
                nc.vector.reciprocal(recips[:, :], safe[:, :]).then_inc(s_recips, 1)

            def scale_edges(i, c):
                dve.wait_ge(s_recips, nth(i, c))
                nc.vector.scalar_tensor_tensor(out=dn[:, :], in0=sums[:, 2:4], scalar=0.0, in1=recips[:, 2:4],
                                               op0=ALU.is_gt, op1=ALU.mult).then_inc(s_dn, 1)
                dve.wait_ge(s_dn, nth(i, c))
                nc.vector.tensor_tensor(edges_dn[:, :], edges[:, :], dn[:, :].unsqueeze(2).to_broadcast([P, 2, P]),
                                        ALU.mult).then_inc(s_prep, 1)

            def invert_counts(i, c):
                dve.wait_ge(s_adj_ps, nth(i, c))
                nc.vector.tensor_scalar(counts[:, :], ps_edges_t[:, :, P], 1.0, None, ALU.max).then_inc(s_counts, 1)
                dve.wait_ge(s_counts, nth(i, c))
                nc.vector.reciprocal(be[:, :], counts[:, :]).then_inc(s_be, 1)

            def gather(i, c, pre, stats, s_pre, s_stats):
                for g in range(2):
                    dve.wait_ge(s_pre, nth(i, c, 2, g))
                    nc.vector.bn_stats(stats[:, g], pre[:, g]).then_inc(s_stats, 1)
                dve.wait_ge(s_stats, nth(i, c, 2, 1))

            def merge(i, c, stats, mv, veps, s_mv, s_veps):
                for g in range(2):
                    nc.vector.bn_aggr(mv[:, g], stats[:, g]).then_inc(s_mv, 1)
                dve.wait_ge(s_mv, nth(i, c, 2, 1))
                nc.vector.tensor_scalar(veps[:, :], mv[:, :, 1], EPS_LN, None, ALU.add).then_inc(s_veps, 1)

            def low_h(i, c, b):
                dve.wait_ge(s_h_hi, nth(i, c, 2, b))
                part = slice(2 * b, 2 * b + 2)
                nc.vector.tensor_tensor(h_split[LOW][:, part], h[:, part], h_split[HIGH][:, part].bitcast(fp32),
                                        ALU.subtract).then_inc(s_h_lo, 1)

            def low_yb(i, c, g):
                dve.wait_ge(s_yb_hi, nth(i, c, 2, g))
                nc.vector.tensor_tensor(yb[LOW][:, g], ps_y[g][:, D:2 * D], yb[HIGH][:, g].bitcast(fp32),
                                        ALU.subtract).then_inc(s_yb, 1)

            def scale_q(i, c):
                for g in range(2):
                    nc.vector.scalar_tensor_tensor(
                        out=q_sb[:, g], in0=ps_q[g][:, 0:D], scalar=rstd_h[:, g:g + 1], in1=beta_w2[:, :],
                        op0=ALU.mult, op1=ALU.add).then_inc(s_q, 1)

            def add_residual(i, c):
                dve.wait_ge(s_x1_b2, nth(i, c, 2, 1))
                if later(i, c, 2):
                    dve.wait_ge(s_out, nth(i, c - 2, 2, 1))
                for g in range(2):
                    dve.wait_ge(s_f_ps, nth(i, c, 2, g))
                    nc.vector.scalar_tensor_tensor(
                        out=pre2[:, c % 2, g], in0=x1_b2[:, c % 2, g], scalar=2.0, in1=ps_f[g],
                        op0=ALU.mult, op1=ALU.add).then_inc(s_pre2, 1)

            def low_u(i, c):
                low_part(u_t, ps_u_t[:, :], s_u_hi, s_u_t, nth(i, c))

            def step(i, c):
                if live(i, c):
                    low_yb(i, c, 0)
                if live(i, c - 2):
                    dve.wait_ge(s_rstd_h, nth(i, c - 2))
                    if splits_q(i, c - 3) and later(i, c - 2, 1):
                        dve.wait_ge(s_q_lo, nth(i, c - 3, 2, 1))
                    elif is_drain(i, c - 1):
                        dve.wait_ge(s_f_ps, nth(i, c - 3, 2, 1))
                    scale_q(i, c - 2)
                if live(i, c):
                    low_yb(i, c, 1)
                if is_last(i, c - 2):
                    gather(i, c - 3, pre2[:, (c - 3) % 2], stats2, s_pre2, s_stats2)
                if is_step(i, c, 0):
                    invert_counts(0, 0)
                    sum_adj(0, 1)
                    invert_sums(0, 1)
                if live(i, c - 3):
                    if is_last(i, c - 3):
                        dve.wait_ge(s_shift2, nth(i, c - 4))
                    merge(i, c - 3, stats2, mv2, veps2, s_mv2, s_veps2)
                if live(i, c + 1):
                    scale_edges(i, c + 1)
                if live(i, c):
                    dve.wait_ge(s_x_in[c % 2], loads(i, c))
                    for g in range(2):
                        dve.wait_ge(s_p_ps, nth(i, c, 2, g))
                        nc.vector.scalar_tensor_tensor(
                            out=pre1[:, g], in0=ps_y[g][:, 0:D], scalar=0.0, in1=x_sb[:, c % 2, g],
                            op0=ALU.max, op1=ALU.add).then_inc(s_pre1, 1)
                    gather(i, c, pre1, stats1, s_pre1, s_stats1)
                if live(i, c + 1):
                    low_part(x_t, ps_x_t[:, :], s_x_hi, s_x_t, nth(i, c + 1))
                if live(i, c):
                    merge(i, c, stats1, mv1, veps1, s_mv1, s_veps1)
                if live(i, c - 1):
                    low_h(i, c - 1, 0)
                if is_step(i, c, 0):
                    dve.wait_ge(s_vectors_in, 16 * 4)
                    nc.vector.tensor_scalar(b2_half[:, :], b2_rows[:, :], 0.5, None, ALU.mult).then_inc(s_b2_half, 1)
                if live(i, c):
                    dve.wait_ge(s_rstd1, nth(i, c))
                    if later(i, c, 1):
                        dve.wait_ge(s_x1_b2, nth(i, c - 1, 2, 1))
                    for g in range(2):
                        nc.vector.tensor_scalar(x1[:, g], pre1[:, g], mv1[:, g, 0:1], rstd1[:, g:g + 1],
                                                ALU.subtract, ALU.mult).then_inc(s_x1, 1)
                if live(i, c - 1):
                    low_h(i, c - 1, 1)
                if live(i, c + 1):
                    invert_counts(i, c + 1)
                if is_last(i, c - 1):
                    sum_squares(nc.vector, dve, i, c - 1)
                if live(i, c - 2) and not is_last(i, c - 1):
                    add_residual(i, c - 2)
                    gather(i, c - 2, pre2[:, c % 2], stats2, s_pre2, s_stats2)
                if live(i, c - 3):
                    dve.wait_ge(s_rstd2, nth(i, c - 3))
                    nc.vector.scalar_tensor_tensor(out=shift2[:, (c - 3) % 2], in0=mv2[:, :, 0], scalar=-1.0,
                                                   in1=rstd2[:, (c - 3) % 2],
                                                   op0=ALU.mult, op1=ALU.mult).then_inc(s_shift2, 1)
                if is_last(i, c - 3):
                    dve.wait_ge(s_stored[(c - 3) % 2], loads(i, c - 5))
                    dve.wait_ge(s_out, nth(i, c - 4, 2, 1))
                    nc.vector.tensor_scalar(out_sb[:, (c - 3) % 2, 1], pre2[:, (c - 3) % 2, 1], mv2[:, 1, 0:1],
                                            rstd2[:, (c - 3) % 2, 1:2], ALU.subtract, ALU.mult).then_inc(s_out, 1)
                if live(i, c + 2):
                    sum_adj(i, c + 2)
                if is_last(i, c):
                    low_u(i, c)
                if live(i, c - 1):
                    dve.wait_ge(s_q_ps, nth(i, c - 1))
                    for g in range(2):
                        nc.vector.tensor_copy(hsum[:, g], ps_q[g][:, D:D + 3:2]).then_inc(s_hsum, 1)
                if live(i, c + 2):
                    invert_sums(i, c + 2)
                if live(i, c - 1):
                    dve.wait_ge(s_hsum, nth(i, c - 1, 2, 1))
                    nc.vector.scalar_tensor_tensor(out=mean_sq[:, :], in0=hsum[:, :, 0], scalar=1.0 / HID ** 2,
                                                   in1=hsum[:, :, 0], op0=ALU.mult, op1=ALU.mult).then_inc(s_mean_sq, 1)
                    dve.wait_ge(s_mean_sq, nth(i, c - 1))
                    nc.vector.scalar_tensor_tensor(out=var_h[:, :], in0=hsum[:, :, 1], scalar=1.0 / HID,
                                                   in1=mean_sq[:, :], op0=ALU.mult, op1=ALU.subtract).then_inc(s_var_h, 1)
                    dve.wait_ge(s_var_h, nth(i, c - 1))
                    nc.vector.tensor_scalar(veps_h[:, :], var_h[:, :], 0.0, EPS_LN, ALU.max, ALU.add).then_inc(s_veps_h, 1)
                if is_last(i, c - 1):
                    add_residual(i, c - 2)
                if is_step(i, c, 0):
                    centre_w2()
                if live(i, c) and not is_last(i, c):
                    low_u(i, c)

            dve.wait_ge(s_consts, CONSTS)
            low_part(x_t, ps_x_t[:, :], s_x_hi, s_x_t, 1)
            sum_adj(0, 0)
            low_parts(0, wab, ps_y)
            invert_sums(0, 0)
            scale_edges(0, 0)
            low_parts(1, w1t, ps_z)
            run(dve, step)

        @block.tensor
        def _(pe):
            mm = nc.tensor.matmul
            pe.wait_ge(s_consts, CONSTS)

            def turn_weights(n, jobs):
                pe.wait_ge(s_w_in[n], 16)
                for dst, blocks in jobs:
                    for b, src in enumerate(blocks):
                        last = nc.tensor.transpose(dst[:, b * P:(b + 1) * P], src, ident[:, :])
                    last.then_inc(s_w_ps[n], 1)

            def turn_w0():
                turn_weights(0, [(ps_y[k], [w0_raw[:, b, f * D + k * P:f * D + (k + 1) * P]
                                            for f in range(2) for b in range(D // P)]) for k in range(KD)])

            def turn_w1():
                turn_weights(1, [(ps_z[k], [w1_raw[:, b, k * P:(k + 1) * P] for b in range(KH)]) for k in range(KD)])

            def turn_w2():
                pe.wait_ge(s_w_lo[1], KD)
                turn_weights(2, [(bank[6 + j], [w2_raw[:, b, k * P:(k + 1) * P] for k in (2 * j, 2 * j + 1)
                                            for b in range(D // P)]) for j in range(2)])

            def reduce_w2():
                pe.wait_ge(s_wide, 1)
                pe.wait_ge(s_w2t, 2)
                for k in range(KH):
                    last = mm(bank[7][:, 0:D], beta_wide[:, k, :], w2t[:, k, :], start=(k == 0), stop=(k == KH - 1))
                last.then_inc(s_beta_ps, 1)
                pe.wait_ge(s_wide, 2)
                for k in range(KH):
                    last = mm(bank[6][:, 0:D], gamma_wide[:, k, :], w2t[:, k, :], start=(k == 0), stop=(k == KH - 1))
                last.then_inc(s_sum_ps, 1)

            def turn_x(i, c):
                slot = c % 2
                pe.wait_ge(s_x_in[slot], loads(i, c))
                if later(i, c, 1):
                    pe.wait_ge(s_x_t, nth(i, c - 1))
                for g in range(2):
                    for k in range(KD):
                        last = nc.tensor.transpose(ps_x_t[:, (g * KD + k) * P:(g * KD + k + 1) * P],
                                                   x_sb[:, slot, g, k * P:(k + 1) * P], ident[:, :])
                last.then_inc(s_x_ps, 1)

            def turn_adj(i, c):
                pe.wait_ge(s_prep, nth(i, c, 2, 1))
                pe.wait_ge(s_adj_n, nth(i, c, 2, 1))
                if later(i, c, 1):
                    pe.wait_ge(s_edn_t, nth(i, c - 1))
                    pe.wait_ge(s_ebe_t, nth(i, c - 1, 2, 1))
                for g in range(2):
                    nc.tensor.transpose(ps_adj_t[:, g * P:(g + 1) * P], adj_n[:, g], ident[:, :])
                    nc.tensor.transpose(ps_edn_t[:, g * P:(g + 1) * P], edges_dn[:, g], ident[:, :])
                for g in range(2):
                    last = mm(ps_edges_t[:, g, 0:P + 2], edges[:, g], ident_ones[:, :], start=True, stop=True)
                last.then_inc(s_adj_ps, 1)

            def product(dst, blocks, left, right, added=False):
                for n, (a, b) in enumerate(PASSES):
                    for k in range(blocks):
                        last = mm(dst, left(a, k), right(b, k), start=(n == 0 and k == 0 and not added),
                                  stop=(n == len(PASSES) - 1 and k == blocks - 1), skip_group_check=added)
                return last

            def move_u(i, c):
                pe.wait_ge(s_g, nth(i, c))
                for g in range(2):
                    pe.wait_ge(s_x1, nth(i, c, 2, g))
                    for k in range(KD):
                        last = mm(ps_u_t[:, (k * 2 + g) * P:(k * 2 + g + 1) * P], x1[:, g, k * P:(k + 1) * P],
                                  g_sb[:, c % 2, g, :], start=True, stop=True)
                last.then_inc(s_u_ps, 1)

            def step(i, c):
                if live(i, c):
                    pe.wait_ge(s_x_t, nth(i, c))
                    for g in range(2):
                        if later(i, c, 1):
                            pe.wait_ge(s_pre1, nth(i, c - 1, 2, g))
                        if later(i, c, 3):
                            pe.wait_ge(s_pre2, nth(i, c - 3, 2, g))
                        last = product(ps_y[g][:, :], KD, lambda a, k: x_t[a][:, g, k, :], lambda b, k: wab[b][:, k, :])
                        last.then_inc(s_y_ps, 1)
                if is_step(i, c, 0):
                    turn_adj(0, 0)
                    turn_w2()
                if live(i, c + 1):
                    turn_x(i, c + 1)
                if live(i, c):
                    pe.wait_ge(s_ebe_t, nth(i, c, 2, 1))
                    pe.wait_ge(s_edn_t, nth(i, c))
                    if later(i, c, 1):
                        pe.wait_ge(s_u_t, nth(i, c - 1))
                    for g in range(2):
                        last = mm(ps_g[:, g * P:(g + 1) * P], edges_be_t[:, g, :], edges_dn_t[:, g, :],
                                  start=True, stop=True)
                    last.then_inc(s_g_ps, 1)
                if live(i, c):
                    pe.wait_ge(s_adj_lo, nth(i, c))
                    for g in range(2):
                        pe.wait_ge(s_yb, nth(i, c, 2, g))
                        product(ps_y[g][:, 0:D], 1, lambda a, k: adj_t_split[a][:, c % 2, g, :],
                                lambda b, k: yb[b][:, g, :], added=True).then_inc(s_p_ps, 1)
                if live(i, c - 1):
                    if is_step(i, c, 1):
                        pe.wait_ge(s_beta_w2, 1)
                        pe.wait_ge(s_centred, 1)
                    pe.wait_ge(s_u_t, nth(i, c - 1))
                    if later(i, c - 1, 1) and z_banks(i, c - 1) is ps_z:
                        pe.wait_ge(s_q, nth(i, c - 2, 2, 1))
                    for m in range(KH):
                        last = product(z_banks(i, c - 1)[m // 2][:, (m % 2) * 2 * P:(m % 2 + 1) * 2 * P], KD,
                                       lambda a, k: w1t[a][:, k, m * P:(m + 1) * P], lambda b, k: u_t[b][:, k])
                        last.then_inc(s_z_ps, 1)
                if splits_q(i, c - 2):
                    for g in range(2):
                        pe.wait_ge(s_g_lo, nth(i, c - 2))
                        pe.wait_ge(s_q_lo, nth(i, c - 2, 2, g))
                        pe.wait_ge(s_pre1, nth(i, c, 2, g))
                        product(ps_f[g], 1, lambda a, k: g_split[a][:, c % 2, g, :], lambda b, k: q_split[b][:, g, :])\
                            .then_inc(s_f_ps, 1)
                if is_step(i, c, 0):
                    reduce_w2()
                if live(i, c + 1):
                    turn_adj(i, c + 1)
                if live(i, c - 1):
                    if is_step(i, c, 1):
                        pe.wait_ge(s_w_lo[2], 1)
                    for order in H_ORDER:
                        if is_last(i, c) and order is H_ORDER[1]:
                            move_u(i, c)
                        for g in range(2):
                            if is_drain(i, c) and order is H_ORDER[0]:
                                pe.wait_ge(s_q, nth(i, c - 2, 2, g))
                            if g == 1 and order is H_ORDER[0]:
                                pe.wait_ge(s_h, nth(i, c - 1, KH, KH - 1))
                            for part, m in order:
                                if g == 0 and m % 2 == 0:
                                    pe.wait_ge((s_h_hi, s_h_lo)[part], nth(i, c - 1, 2, m // 2))
                                for other in ((HIGH, LOW) if part == HIGH else (HIGH,)):
                                    mm(ps_q[g][:, 0:D + 2], h_split[part][:, m, g, :], w2c[other][:, m, :],
                                       start=((part, m, other) == (HIGH, 0, HIGH)), stop=((part, m) == H_ORDER[-1][-1]))
                if live(i, c) and not is_last(i, c):
                    move_u(i, c)
                if live(i, c - 1):
                    pe.wait_ge(s_h_sq1, nth(i, c - 1))
                    for g in range(2):
                        last = mm(ps_q[g][:, STAT:STAT + 1], h_sq1[:, g, :], ones_col[:, 0:1], start=True, stop=True)
                    last.then_inc(s_q_ps, 1)
                if is_drain(i, c) and live(i, c - 2):
                    for g in range(2):
                        pe.wait_ge(s_q, nth(i, c - 2, 2, g))
                        if live(i, c - 3):
                            pe.wait_ge(s_pre2, nth(i, c - 3, 2, g))
                        mm(ps_f[g], g_sb[:, c % 2, g, :], q_sb[:, g, :], start=True, stop=True).then_inc(s_f_ps, 1)

            turn_x(0, 0)
            turn_w0()
            turn_w1()
            pe.wait_ge(s_w_lo[0], KD)
            run(pe, step)


_INS = ['x', 'adj', 'L0_gnn_W', 'L1_gnn_W1', 'L1_gnn_b1', 'L1_gnn_gamma', 'L1_gnn_beta', 'L1_gnn_W2', 'L1_gnn_b2']
_OUTS = [((64, 128, 256), 'float32')]


def kernel(**inputs):
    import numpy as _np
    import concourse.bacc as _bacc
    from concourse import mybir as _mybir
    from concourse.bass_utils import run_bass_kernel_spmd as _run

    nc = _bacc.Bacc("TRN2", target_bir_lowering=False, num_devices=1)
    arrays, args = {}, []
    for name in _INS:
        a = _np.ascontiguousarray(inputs[name])
        arrays[f"in_{name}_dram"] = a
        args.append(nc.dram_tensor(f"in_{name}_dram", a.shape, _mybir.dt.from_np(a.dtype), kind="ExternalInput").ap())
    for i, (shape, dtype) in enumerate(_OUTS):
        dt = _mybir.dt.from_np(_np.dtype(dtype))
        args.append(nc.dram_tensor(f"out_{i}_dram", shape, dt, kind="ExternalOutput").ap())
    gnn_hypergraph_kernel(nc, *args)
    r = _run(nc, [arrays], core_ids=[0])
    got = tuple(r.results[0][f"out_{i}_dram"] for i in range(len(_OUTS)))
    return got[0]
```
